# Optimizing a Trainium2 kernel written in Bass

```python
import numpy as np
import jax
import jax.numpy as jnp

def _softmax(x, axis=-1):
    return jax.nn.softmax(x, axis=axis)

def _gelu(x):
    return jax.nn.gelu(x, approximate=True)

def _silu(x):
    return jax.nn.silu(x)

def _sigmoid(x):
    return jax.nn.sigmoid(x)

def _layernorm(x, axis=-1, eps=1e-05):
    m = jnp.mean(x, axis=axis, keepdims=True)
    v = jnp.var(x, axis=axis, keepdims=True)
    return (x - m) / jnp.sqrt(v + eps)

def _scatter_add(tgt, idx, src, axis=0):
    return tgt.at[idx].add(src)

def _segment_sum(src, seg, n):
    return jax.ops.segment_sum(src, seg, n)
kernel_name = 'mk_adaln_d1_jaxref_r4_538580'

def setup_inputs(seed: int=0):
    np.random.seed(seed)
    _w = jnp.asarray

    def _L0_attn_setup():
        import jax, jax.numpy as jnp
        import numpy as np
        D_MODEL = 256
        N_HEADS = 16
        WINDOW = 64
        S_DIM = 128
        BATCH = 1
        SEQ = 1024
        EPS = 1e-05

        def _layernorm(x, g, b):
            mu = jnp.mean(x, -1, keepdims=True)
            var = jnp.mean((x - mu) ** 2, -1, keepdims=True)
            return (x - mu) * jax.lax.rsqrt(var + EPS) * g + b

        def _windowed_attn(xn, W_qkv, W_O, b_O):
            Bq, T, d = xn.shape
            H, Dh, C = (N_HEADS, d // N_HEADS, WINDOW)
            N = T // C
            qkv = xn @ W_qkv
            q, k, v = jnp.split(qkv, 3, axis=-1)

            def blk(t):
                return t.reshape(Bq, T, H, Dh).transpose(0, 2, 1, 3).reshape(Bq, H, N, C, Dh)
            Qb, Kb, Vb = (blk(q), blk(k), blk(v))

            def win(t):
                prev = jnp.concatenate([jnp.zeros_like(t[:, :, :1]), t[:, :, :-1]], axis=2)
                return jnp.concatenate([prev, t], axis=3)
            Kw, Vw = (win(Kb), win(Vb))
            scores = jnp.einsum('bhncd,bhnkd->bhnck', Qb, Kw) / np.sqrt(Dh).astype(np.float32)
            qi = jnp.arange(C)[:, None]
            kk = jnp.arange(2 * C)[None, :]
            band = (kk > qi) & (kk <= qi + C)
            mask = jnp.where((jnp.arange(N) == 0)[:, None, None], band & (kk >= C), band)
            scores = jnp.where(mask[None, None], scores, -jnp.inf)
            p = jax.nn.softmax(scores, axis=-1)
            o = jnp.einsum('bhnck,bhnkd->bhncd', p, Vw)
            o = o.reshape(Bq, H, T, Dh).transpose(0, 2, 1, 3).reshape(Bq, T, d)
            return o @ W_O + b_O
        key = jax.random.key(seed)
        ks = jax.random.split(key, 10)
        d, s = (D_MODEL, S_DIM)

        def w(k, shape, fan_in):
            return jax.random.normal(k, shape, jnp.float32) * fan_in ** (-0.5)
        return {'x': jax.random.normal(ks[0], (BATCH, SEQ, d), jnp.float32), 'ln1_g': jnp.ones((d,), jnp.float32), 'ln1_b': jnp.zeros((d,), jnp.float32), 'ln2_g': jnp.ones((d,), jnp.float32), 'ln2_b': jnp.zeros((d,), jnp.float32), 'W_qkv': w(ks[1], (d, 3 * d), d), 'W_O': w(ks[2], (d, d), d), 'b_O': jnp.zeros((d,), jnp.float32), 'W_ug': w(ks[3], (d, s + d), d), 'b_ug': jnp.zeros((s + d,), jnp.float32), 'B_w': w(ks[4], (d, s), d), 'A': jax.random.uniform(ks[5], (s,), jnp.float32, -0.1, 0.1), 'C_w': w(ks[6], (s, d), s), 'mlp_W1': w(ks[7], (d, 4 * d), d), 'mlp_b1': jnp.zeros((4 * d,), jnp.float32), 'mlp_W2': w(ks[8], (4 * d, d), 4 * d), 'mlp_b2': jnp.zeros((d,), jnp.float32)}
    _L0_attn_in = _L0_attn_setup()

    def _L0_ffn_setup():
        import jax, jax.numpy as jnp
        import numpy as np
        ALPHA = 1.702
        LIMIT = 9.0
        TOP_K = 2

        def swiglu(x):
            g, v = (x[..., 0::2], x[..., 1::2])
            g = jnp.clip(g, None, LIMIT)
            v = jnp.clip(v, -LIMIT, LIMIT)
            return g * jax.nn.sigmoid(ALPHA * g) * (v + 1)
        key = jax.random.key(seed)
        ks = jax.random.split(key, 6)
        B, L, D = (2, 512, 256)
        E, F = (8, 512)
        s_gate = 1.0 / np.sqrt(D)
        s1 = 1.0 / np.sqrt(D)
        s2 = 1.0 / np.sqrt(F)
        return {'x': jax.random.normal(ks[0], (B, L, D), dtype=jnp.float32), 'gate_w': jax.random.normal(ks[1], (D, E), dtype=jnp.float32) * s_gate, 'dense_1_w': jax.random.normal(ks[2], (E, 2 * F, D), dtype=jnp.float32) * s1, 'dense_1_b': jnp.zeros((E, 2 * F), dtype=jnp.float32), 'dense_2_w': jax.random.normal(ks[3], (E, D, F), dtype=jnp.float32) * s2, 'dense_2_b': jnp.zeros((E, D), dtype=jnp.float32)}
    _L0_ffn_in = _L0_ffn_setup()
    _L0_c = _w((lambda *s: np.random.randn(*s).astype(np.float32) * 0.05)(16, 256))
    _L0_wmod = _w((lambda *s: np.random.randn(*s).astype(np.float32) * 0.05)(256, 6 * 256) * 256 ** (-0.5))
    _d = {'L0_attn_x': _L0_attn_in['x'], 'L0_attn_ln1_g': _L0_attn_in['ln1_g'], 'L0_attn_ln1_b': _L0_attn_in['ln1_b'], 'L0_attn_ln2_g': _L0_attn_in['ln2_g'], 'L0_attn_ln2_b': _L0_attn_in['ln2_b'], 'L0_attn_W_qkv': _L0_attn_in['W_qkv'], 'L0_attn_W_O': _L0_attn_in['W_O'], 'L0_attn_b_O': _L0_attn_in['b_O'], 'L0_attn_W_ug': _L0_attn_in['W_ug'], 'L0_attn_b_ug': _L0_attn_in['b_ug'], 'L0_attn_B_w': _L0_attn_in['B_w'], 'L0_attn_A': _L0_attn_in['A'], 'L0_attn_C_w': _L0_attn_in['C_w'], 'L0_attn_mlp_W1': _L0_attn_in['mlp_W1'], 'L0_attn_mlp_b1': _L0_attn_in['mlp_b1'], 'L0_attn_mlp_W2': _L0_attn_in['mlp_W2'], 'L0_attn_mlp_b2': _L0_attn_in['mlp_b2'], 'L0_ffn_gate_w': _L0_ffn_in['gate_w'], 'L0_ffn_dense_1_w': _L0_ffn_in['dense_1_w'], 'L0_ffn_dense_1_b': _L0_ffn_in['dense_1_b'], 'L0_ffn_dense_2_w': _L0_ffn_in['dense_2_w'], 'L0_ffn_dense_2_b': _L0_ffn_in['dense_2_b'], 'L0_c': _L0_c, 'L0_wmod': _L0_wmod}
    _x0 = _d['L0_attn_x']
    _d['L0_attn_x'] = jax.random.normal(jax.random.fold_in(jax.random.key(seed), 1), (16, 512, 256), dtype=_x0.dtype)
    del _x0
    return _d

def reference(L0_attn_x, L0_attn_ln1_g, L0_attn_ln1_b, L0_attn_ln2_g, L0_attn_ln2_b, L0_attn_W_qkv, L0_attn_W_O, L0_attn_b_O, L0_attn_W_ug, L0_attn_b_ug, L0_attn_B_w, L0_attn_A, L0_attn_C_w, L0_attn_mlp_W1, L0_attn_mlp_b1, L0_attn_mlp_W2, L0_attn_mlp_b2, L0_ffn_gate_w, L0_ffn_dense_1_w, L0_ffn_dense_1_b, L0_ffn_dense_2_w, L0_ffn_dense_2_b, L0_c, L0_wmod):

    def _L0_attn_ref(x, ln1_g, ln1_b, ln2_g, ln2_b, W_qkv, W_O, b_O, W_ug, b_ug, B_w, A, C_w, mlp_W1, mlp_b1, mlp_W2, mlp_b2):
        import jax, jax.numpy as jnp
        import numpy as np
        D_MODEL = 256
        N_HEADS = 16
        WINDOW = 64
        S_DIM = 128
        BATCH = 1
        SEQ = 1024
        EPS = 1e-05

        def _layernorm(x, g, b):
            mu = jnp.mean(x, -1, keepdims=True)
            var = jnp.mean((x - mu) ** 2, -1, keepdims=True)
            return (x - mu) * jax.lax.rsqrt(var + EPS) * g + b

        def _windowed_attn(xn, W_qkv, W_O, b_O):
            Bq, T, d = xn.shape
            H, Dh, C = (N_HEADS, d // N_HEADS, WINDOW)
            N = T // C
            qkv = xn @ W_qkv
            q, k, v = jnp.split(qkv, 3, axis=-1)

            def blk(t):
                return t.reshape(Bq, T, H, Dh).transpose(0, 2, 1, 3).reshape(Bq, H, N, C, Dh)
            Qb, Kb, Vb = (blk(q), blk(k), blk(v))

            def win(t):
                prev = jnp.concatenate([jnp.zeros_like(t[:, :, :1]), t[:, :, :-1]], axis=2)
                return jnp.concatenate([prev, t], axis=3)
            Kw, Vw = (win(Kb), win(Vb))
            scores = jnp.einsum('bhncd,bhnkd->bhnck', Qb, Kw) / np.sqrt(Dh).astype(np.float32)
            qi = jnp.arange(C)[:, None]
            kk = jnp.arange(2 * C)[None, :]
            band = (kk > qi) & (kk <= qi + C)
            mask = jnp.where((jnp.arange(N) == 0)[:, None, None], band & (kk >= C), band)
            scores = jnp.where(mask[None, None], scores, -jnp.inf)
            p = jax.nn.softmax(scores, axis=-1)
            o = jnp.einsum('bhnck,bhnkd->bhncd', p, Vw)
            o = o.reshape(Bq, H, T, Dh).transpose(0, 2, 1, 3).reshape(Bq, T, d)
            return o @ W_O + b_O
        xn = _layernorm(x, ln1_g, ln1_b)
        attn = _windowed_attn(xn, W_qkv, W_O, b_O)
        ug = xn @ W_ug + b_ug
        u = ug[..., :S_DIM]
        g = jax.nn.sigmoid(ug[..., S_DIM:])
        drive = xn @ B_w + u

        def step(s, ut):
            s2 = A * s + ut
            return (s2, s2)
        s0 = jnp.zeros((x.shape[0], S_DIM), x.dtype)
        _, states = jax.lax.scan(step, s0, drive.transpose(1, 0, 2))
        y_ssm = jnp.einsum('tbs,sd->btd', states, C_w)
        x = x + g * attn + (1.0 - g) * y_ssm
        h = _layernorm(x, ln2_g, ln2_b)
        x = x + jax.nn.gelu(h @ mlp_W1 + mlp_b1, approximate=False) @ mlp_W2 + mlp_b2
        return x

    def _L0_ffn_ref(x, gate_w, dense_1_w, dense_1_b, dense_2_w, dense_2_b):
        import jax, jax.numpy as jnp
        import numpy as np
        ALPHA = 1.702
        LIMIT = 9.0
        TOP_K = 2

        def swiglu(x):
            g, v = (x[..., 0::2], x[..., 1::2])
            g = jnp.clip(g, None, LIMIT)
            v = jnp.clip(v, -LIMIT, LIMIT)
            return g * jax.nn.sigmoid(ALPHA * g) * (v + 1)
        B, L, D = x.shape
        xf = x.reshape(B * L, D)
        gate = xf @ gate_w
        weights, sel = jax.lax.top_k(gate, k=TOP_K)
        weights = jax.nn.softmax(weights, axis=-1)
        h = jnp.einsum('ecd,td->tec', dense_1_w, xf) + dense_1_b[None]
        h = swiglu(h)
        y = jnp.einsum('edf,tef->ted', dense_2_w, h) + dense_2_b[None]
        y_sel = jnp.take_along_axis(y, sel[:, :, None], axis=1)
        out = jnp.einsum('tkd,tk->td', y_sel, weights)
        return out.reshape(B, L, D)
    x = L0_attn_x
    mod = (_silu(L0_c) @ L0_wmod).reshape(L0_c.shape[0], 6, 1, -1)
    sa, ca, ga, sb, cb, gb = (mod[:, 0], mod[:, 1], mod[:, 2], mod[:, 3], mod[:, 4], mod[:, 5])
    ga = (2 * (ga >= 0) - 1) * jnp.maximum(jnp.abs(ga), 0.25)
    gb = (2 * (gb >= 0) - 1) * jnp.maximum(jnp.abs(gb), 0.25)
    h = _layernorm(x, axis=-1) * (1 + ca) + sa
    x = x + ga * _L0_attn_ref(h, L0_attn_ln1_g, L0_attn_ln1_b, L0_attn_ln2_g, L0_attn_ln2_b, L0_attn_W_qkv, L0_attn_W_O, L0_attn_b_O, L0_attn_W_ug, L0_attn_b_ug, L0_attn_B_w, L0_attn_A, L0_attn_C_w, L0_attn_mlp_W1, L0_attn_mlp_b1, L0_attn_mlp_W2, L0_attn_mlp_b2)
    h = _layernorm(x, axis=-1) * (1 + cb) + sb
    x = x + gb * _L0_ffn_ref(h, L0_ffn_gate_w, L0_ffn_dense_1_w, L0_ffn_dense_1_b, L0_ffn_dense_2_w, L0_ffn_dense_2_b)
    return x

_drawn_inputs = setup_inputs


def setup_inputs(seed=0):
    import zlib

    import numpy as np

    out = dict(_drawn_inputs(seed))
    spreads = {'L0_attn_ln1_g': (1.0, 0.2),
     'L0_attn_ln1_b': (0.0, 0.1),
     'L0_attn_ln2_g': (1.0, 0.2),
     'L0_attn_ln2_b': (0.0, 0.358),
     'L0_attn_b_O': (0.0, 0.39),
     'L0_attn_b_ug': (0.0, 0.339),
     'L0_attn_mlp_b1': (0.0, 0.375),
     'L0_attn_mlp_b2': (0.0, 0.1),
     'L0_ffn_dense_1_b': (0.0, 0.395),
     'L0_ffn_dense_2_b': (0.0, 0.47)}
    factors = {'L0_attn_A': 2.945}
    for name, (base, spread) in spreads.items():
        noise = np.random.default_rng([zlib.crc32(name.encode()), seed]).standard_normal(out[name].shape)
        drawn = base * np.exp(spread * noise) if base else spread * noise
        out[name] = jnp.asarray(drawn.astype(out[name].dtype))
    for name, factor in factors.items():
        out[name] = (out[name] * factor).astype(out[name].dtype)
    return out
```

```python
from contextlib import ExitStack

import concourse.bass as bass
from concourse import mybir

ALU = mybir.AluOpType
ACT = mybir.ActivationFunctionType
AX = mybir.AxisListType
F32 = mybir.dt.float32
F16 = mybir.dt.float16
BF16 = mybir.dt.bfloat16
I32 = mybir.dt.int32
U32 = mybir.dt.uint32

P = 128
D = 256
KD = D // P
L = 512
TT = L // P
WIN = 64
NW = L // WIN
H = 16
DH = D // H
PAIRS = H // 2
S = 128
FM = 4 * D
FMC = FM // P
E = 8
F = 512
FC = F // P
EPS = 1e-5
MASKED = -1e30
SCALE = DH ** -0.5
SEED, NEWTON = 3, 12
ROWS = 256


class Counter:

    def __init__(self, sem, per):
        self.sem, self.per = sem, per

    def at(self, i, n):
        return max(i * self.per + n, 0) if isinstance(i, int) else i * self.per + n


class Memory:

    def __init__(self, nc, ctx, phase):
        self.nc, self.ctx, self.phase = nc, ctx, phase

    def sb(self, name, shape, dt=F32):
        return self.ctx.enter_context(self.nc.sbuf_tensor(self.phase + name, shape, dt))

    def ps(self, name, shape, dt=F32):
        return self.ctx.enter_context(self.nc.psum_tensor(self.phase + name, shape, dt))

    def counter(self, name, per=1):
        return Counter(self.ctx.enter_context(self.nc.semaphore(self.phase + name)), per)


def wait_alone(eng, sem, value, passed):
    eng.wait_ge(sem, value).then_inc(passed.sem, 1)


def seed_inverse_root(dve, sig, i, n, var, v, y):
    dve.tensor_scalar(v, var, EPS, None, ALU.add).then_inc(sig.sem, 1)
    dve.wait_ge(sig.sem, sig.at(i, n + 1))
    dve.tensor_scalar(y.bitcast(I32), v.bitcast(I32), 1, None, ALU.logical_shift_right).then_inc(sig.sem, 1)
    dve.wait_ge(sig.sem, sig.at(i, n + 2))
    dve.tensor_scalar(y.bitcast(I32), y.bitcast(I32), -1.0, float(0x5F3759DF), ALU.mult, ALU.add
                      ).then_inc(sig.sem, 1)


def refine_inverse_root(pool, sig, i, n, v, y, a, passed):
    for _ in range(3):
        for op in (lambda: pool.tensor_tensor(a, y, y, ALU.mult),
                   lambda: pool.tensor_tensor(a, a, v, ALU.mult),
                   lambda: pool.tensor_scalar(a, a, -0.5, 1.5, ALU.mult, ALU.add),
                   lambda: pool.tensor_tensor(y, y, a, ALU.mult)):
            op().then_inc(sig.sem, 1)
            n += 1
            wait_alone(pool, sig.sem, sig.at(i, n), passed)


def hi_lo_products(pe, out, lhs, rhs, start, stop):
    pe.matmul(out, lhs[0], rhs[0], start=start, stop=False)
    pe.matmul(out, lhs[0], rhs[1], start=False, stop=False)
    return pe.matmul(out, lhs[1], rhs[0], start=False, stop=stop)



def setup(nc, din, w, scratch):
    NB = din["cT"].shape[2]
    jobs = [
        (w["qk"], din["Wqk"], None), (w["v"], din["Wv"], None), (w["g"], din["Wg"], None),
        (w["drive"], din["Bw"], din["Wu"]), (w["o"], din["WO"], None), (w["c"], din["Cw"], None),
        (w["w1"], din["W1"], None), (w["w2"], din["W2"], None), (w["gate"], din["gate_w"], None),
    ]
    rows = [(w["bg3"], din["b_g"]), (w["bo3"], din["b_O"]), (w["b23"], din["mlp_b2"])]
    with ExitStack() as ctx:
        m = Memory(nc, ctx, "setup_")
        stage = m.sb("stage", [P, 2, 2048])
        added = m.sb("added", [P, 256])
        wmod = m.sb("wmod", [P, KD, 6 * D])
        cT = m.sb("cT", [P, KD, NB])
        th = m.sb("th", [P, KD, NB])
        sc = m.sb("sc", [P, KD, NB])
        mod = m.sb("mod", [NB, 6 * D])
        sgn = m.sb("sgn", [NB, D])
        neg = m.sb("neg", [NB, D])
        maskg = m.sb("maskg", [P, 2, 4])
        brow = m.sb("brow", [1, 3, D])
        parts = m.sb("parts", [1, 3, 3, D], BF16)
        pm = [m.ps(f"pm{i}", [P, 512]) for i in range(3)]
        loaded = m.counter("loaded")
        vloaded = m.counter("vloaded")
        cloaded = m.counter("cloaded")
        bloaded = m.counter("bloaded")
        splitting = m.counter("splitting")
        split = m.counter("split")
        summed = m.counter("summed")
        tanh_c = m.counter("tanh_c")
        silu_c = m.counter("silu_c")
        mod_mm = m.counter("mod_mm")
        mod_sb = m.counter("mod_sb")
        mod_out = m.counter("mod_out")
        bsplit = m.counter("bsplit")
        filled = m.counter("filled")
        grouped = m.counter("grouped")
        shaped = m.counter("shaped")
        copied = m.counter("copied")
        bparts = m.counter("bparts")
        block = ctx.enter_context(nc.Block())

        @block.sync
        def _(sp):
            sp.dma_start(cT[:], din["cT"]).then_inc(cloaded.sem, 16)
            sp.dma_start(wmod[:], din["wmod"].rearrange("(k p) n -> p k n", p=P)).then_inc(cloaded.sem, 16)
            for j, (_, b) in enumerate(rows):
                sp.dma_start(brow[:, j, :], b.rearrange("(a n) -> a n", a=1)).then_inc(bloaded.sem, 16)
            for j, (dst, src, k) in enumerate([
                    (w["g1"], din["ln1_g"], KD), (w["b1"], din["ln1_b"], KD), (w["g2"], din["ln2_g"], KD),
                    (w["b2"], din["ln2_b"], KD), (w["mb1"], din["mlp_b1"], FMC), (w["bu"], din["b_u"], 1),
                    (w["A"], din["A"], 1)]):
                sp.dma_start(dst[:], src).then_inc(vloaded.sem, 16)
            for j, (dst, src, plus) in enumerate(jobs):
                n = dst[0].shape[1] * dst[0].shape[2]
                if j >= 2:
                    sp.wait_ge(split.sem, j - 1)
                view = stage[:, j % 2, 0:n].rearrange("p (k n) -> p k n", k=dst[0].shape[1])
                sp.dma_start(view, src.rearrange("(k p) n -> p k n", p=P)).then_inc(loaded.sem, 16)
                if plus is not None:
                    sp.dma_start(added[:, 0:n].rearrange("p (k n) -> p k n", k=dst[0].shape[1]),
                                 plus.rearrange("(k p) n -> p k n", p=P)).then_inc(loaded.sem, 16)
                sp.wait_ge(loaded.sem, 16 * (j + 1) + (16 if j >= 3 else 0))
            sp.wait_ge(vloaded.sem, 16 * 7)
            sp.wait_ge(bparts.sem, 3)
            for j, (dst, _) in enumerate(rows):
                for q in range(3):
                    sp.dma_start(dst[q:q + 1, :], parts[:, j, q, :]).then_inc(bsplit.sem, 16)
            sp.wait_ge(bsplit.sem, 16 * 9)
            sp.wait_ge(mod_sb.sem, 13)
            sp.dma_start(scratch["mod"], mod[:]).then_inc(mod_out.sem, 16)
            sp.wait_ge(mod_out.sem, 16)

        @block.scalar
        def _(act):
            act.wait_ge(cloaded.sem, 32)
            act.activation(th[:], cT[:], ACT.Tanh, scale=0.5).then_inc(tanh_c.sem, 1)

        @block.tensor
        def _(pe):
            pe.wait_ge(silu_c.sem, 2)
            for n in range(3):
                for k in range(KD):
                    last = pe.matmul(pm[n][0:NB, :], sc[:, k, :], wmod[:, k, n * 512:(n + 1) * 512],
                                     start=(k == 0), stop=(k == KD - 1))
                last.then_inc(mod_mm.sem, 1)

        @block.vector
        def _(dve):
            dve.wait_ge(tanh_c.sem, 1)
            dve.scalar_tensor_tensor(out=sc[:], in0=th[:], scalar=1.0, in1=cT[:], op0=ALU.add,
                                     op1=ALU.mult).then_inc(silu_c.sem, 1)
            dve.wait_ge(silu_c.sem, 1)
            dve.tensor_scalar(sc[:], sc[:], 0.5, None, ALU.mult).then_inc(silu_c.sem, 1)
            for n in range(3):
                dve.wait_ge(mod_mm.sem, n + 1)
                dve.tensor_copy(mod[:, n * 512:(n + 1) * 512], pm[n][0:NB, :]).then_inc(mod_sb.sem, 1)
            for half in range(2):
                dve.wait_ge(mod_sb.sem, 3 + 5 * half)
                scale_, gate_ = (mod[:, (3 * half + i) * D:(3 * half + i + 1) * D] for i in (1, 2))
                dve.tensor_scalar(scale_, scale_, 1.0, None, ALU.add).then_inc(mod_sb.sem, 1)
                dve.tensor_scalar(sgn[:], gate_, 0.0, 2.0, ALU.is_ge, ALU.mult).then_inc(mod_sb.sem, 1)
                dve.tensor_scalar(neg[:], gate_, -1.0, None, ALU.mult).then_inc(mod_sb.sem, 1)
                dve.wait_ge(mod_sb.sem, 6 + 5 * half)
                dve.scalar_tensor_tensor(out=gate_, in0=neg[:], scalar=0.25, in1=gate_, op0=ALU.max,
                                         op1=ALU.max).then_inc(mod_sb.sem, 1)
                dve.wait_ge(mod_sb.sem, 7 + 5 * half)
                dve.scalar_tensor_tensor(out=gate_, in0=sgn[:], scalar=-1.0, in1=gate_, op0=ALU.add,
                                         op1=ALU.mult).then_inc(mod_sb.sem, 1)
            dve.wait_ge(bloaded.sem, 48)
            for q in range(3):
                dve.tensor_copy(parts[:, :, q, :], brow[:]).then_inc(bparts.sem, 1)
                dve.wait_ge(bparts.sem, q + 1)
                if q < 2:
                    dve.tensor_tensor(brow[:], brow[:], parts[:, :, q, :], ALU.subtract).then_inc(shaped.sem, 1)
                    dve.wait_ge(shaped.sem, q + 1)
            for j, (dst, _, plus) in enumerate(jobs):
                hi, lo = dst[0], dst[1]
                k = hi.shape[1]
                n = k * hi.shape[2]
                src = stage[:, j % 2, 0:n].rearrange("p (k n) -> p k n", k=k)
                dve.wait_ge(loaded.sem, 16 * (j + 1) + (16 if j >= 3 else 0))
                if plus is not None:
                    dve.tensor_tensor(src, src, added[:, 0:n].rearrange("p (k n) -> p k n", k=k),
                                      ALU.add).then_inc(summed.sem, 1)
                    dve.wait_ge(summed.sem, 1)
                dve.tensor_copy(hi[:], src).then_inc(splitting.sem, 1)
                dve.wait_ge(splitting.sem, j + 1)
                dve.tensor_tensor(lo[:], src, hi[:], ALU.subtract).then_inc(split.sem, 1)
            dve.wait_ge(grouped.sem, 1)
            dve.tensor_reduce(w["parity"][:], maskg[:], AX.X, ALU.add).then_inc(shaped.sem, 1)
            dve.wait_ge(split.sem, len(jobs))
            for part in range(2):
                dve.tensor_scalar(w["nc"][part][:], w["c"][part][:], -1.0, None, ALU.mult).then_inc(shaped.sem, 1)

        @block.gpsimd
        def _(pool):
            n = 0

            def step(ins):
                nonlocal n
                n += 1
                ins.then_inc(filled.sem, 1)
                pool.wait_ge(filled.sem, n)

            step(pool.memset(w["identf"][:], 1.0))
            step(pool.affine_select(out=w["identf"][:], in_=w["identf"][:], compare_op=ALU.is_equal, fill=0.0,
                                    base=0, pattern=[[-1, P]], channel_multiplier=1))
            for name in ("identb", "identh"):
                step(pool.tensor_copy(w[name][:], w["identf"][:]))
            step(pool.memset(w["ones3"][:], 1.0))
            for name in ("twoI", "maskq", "select", "shift"):
                step(pool.memset(w[name][:], 0.0))
            step(pool.tensor_copy(w["twoI"][0:WIN, 0:WIN], w["identf"][0:WIN, 0:WIN]))
            step(pool.tensor_copy(w["twoI"][0:WIN, WIN:P], w["identf"][0:WIN, 0:WIN]))
            step(pool.memset(maskg[:], 1.0))
            for par in range(2):
                v = maskg[:, par, :]
                step(pool.affine_select(out=v, in_=v, compare_op=ALU.is_ge, fill=0.0, base=-DH * par,
                                        pattern=[[-2 * DH, 4]], channel_multiplier=1))
                step(pool.affine_select(out=v, in_=v, compare_op=ALU.is_ge, fill=0.0, base=DH * par + DH - 1,
                                        pattern=[[2 * DH, 4]], channel_multiplier=-1))
            pool.sem_inc(grouped.sem, 1)
            for var in range(2):
                v = w["maskq"][0:WIN, var, :, :]
                step(pool.affine_select(out=v, in_=v, compare_op=ALU.is_gt, fill=MASKED, base=0,
                                        pattern=[[0, 4], [1, P]], channel_multiplier=-1))
                step(pool.affine_select(out=v, in_=v, compare_op=ALU.is_ge, fill=MASKED, base=WIN,
                                        pattern=[[0, 4], [-1, P]], channel_multiplier=1))
                if var == 1:
                    step(pool.affine_select(out=v, in_=v, compare_op=ALU.is_ge, fill=MASKED, base=-WIN,
                                            pattern=[[0, 4], [1, P]], channel_multiplier=0))
                s = w["select"][0:WIN + PAIRS, var, :, :]
                step(pool.memset(s, -1.0))
                step(pool.affine_select(out=s, in_=s, compare_op=ALU.is_equal, fill=0.0, base=-WIN,
                                        pattern=[[-1, PAIRS], [0, P]], channel_multiplier=1))
                for i in range(PAIRS):
                    step(pool.tensor_copy(w["select"][0:WIN, var, i, :], w["maskq"][0:WIN, var, 0, :]))
            for b in range(2):
                step(pool.tensor_copy(w["shift"][0:WIN, b, :], w["twoI"][0:WIN, :]))
            step(pool.memset(w["before"][:], 1.0))
            step(pool.affine_select(out=w["before"][:], in_=w["before"][:], compare_op=ALU.is_gt, fill=0.0,
                                    base=0, pattern=[[1, P]], channel_multiplier=-1))
            step(pool.memset(w["ones"][:], 1.0))
            for name in ("xTh", "xTl"):
                step(pool.memset(w[name][:, :, 0:WIN], 0.0))
            step(pool.memset(w["Kz"][:].bitcast(F32), 0.0))
            step(pool.memset(w["mx"][:], 0.0))
            step(pool.memset(w["V"][:, :, :, 2 * DH:2 * DH + 1], 1.0))



def mixer(nc, din, w, scratch, NB):
    with ExitStack() as ctx:
        m = Memory(nc, ctx, "mixer_")
        x = m.sb("x", [P, TT, D])
        shsc = m.sb("shsc", [P, 2, D])
        nrm = m.sb("nrm", [P, TT, D])
        h = m.sb("h", [P, TT, D])
        hres = m.sb("hres", [P, TT, D])
        stats = m.sb("stats", [P, TT, 6])
        mv = m.sb("mv", [P, TT, 2])
        ve = m.sb("ve", [P, TT])
        rs = m.sb("rs", [P, TT])
        nt = m.sb("nt", [P, TT])
        xTf = m.sb("xTf", [P, KD, L])
        Qh = m.sb("Qh", [P, 2, NW, 2, WIN], F16)
        Ql = m.sb("Ql", [P, 2, NW, 2, WIN], F16)
        xTh, xTl, V, mx = (w[n] for n in ("xTh", "xTl", "V", "mx"))
        Kt = m.sb("Kt", [P, 2, 2, L], F16)
        Kz = w["Kz"]
        drv = m.sb("drv", [P, L])
        st = m.sb("st", [P, L])
        sth = m.sb("sth", [P, L], F16)
        stl = m.sb("stl", [P, L], F16)
        prob = m.sb("prob", [P, 2, PAIRS * P])
        rden = m.sb("rden", [P, 2, PAIRS])
        on = m.sb("on", [P, 2, PAIRS, DH])
        oTh = m.sb("oTh", [P, 2, L], F16)
        oTl = m.sb("oTl", [P, 2, L], F16)
        mix = m.sb("mix", [P, TT, D])
        x1 = m.sb("x1", [P, TT, D])
        sc = m.ps("sc", [P, 4, 512])
        pj = m.ps("pj", [P, 2, 512])
        pv = m.ps("pv", [P, 512])
        pm = m.ps("pm", [P, P], BF16)

        x_in = m.counter("x_in", 32)
        dve_passed, pool_passed = m.counter("dve_passed"), m.counter("pool_passed")
        s_stats = m.counter("s_stats", 8)
        s_aggr = m.counter("s_aggr", 8)
        s_seed = m.counter("s_seed", 2 * SEED)
        s_rstd = m.counter("s_rstd", 2 * NEWTON)
        s_norm0 = m.counter("s_norm0", 4)
        s_h = m.counter("s_h", 2)
        s_norm1 = m.counter("s_norm1", 4)
        h_kept = m.counter("h_kept", 16)
        xT_mm = m.counter("xT_mm", 2)
        xT_f = m.counter("xT_f", 2)
        xT_hi = m.counter("xT_hi", 2)
        xT_lo = m.counter("xT_lo", 2)
        q_mm = m.counter("q_mm", 2)
        q_hi = m.counter("q_hi", 4)
        q_lo = m.counter("q_lo", 4)
        k_mm = m.counter("k_mm", 2)
        k_hi = m.counter("k_hi", 2)
        k_lo = m.counter("k_lo", 2)
        k_spread = m.counter("k_spread", 64)
        v_mm = m.counter("v_mm", 4)
        v_sb = m.counter("v_sb", 4)
        drive_mm = m.counter("drive_mm", 1)
        drive_sb = m.counter("drive_sb", 1)
        scanned = m.counter("scanned", 1)
        st_hi = m.counter("st_hi", 1)
        st_lo = m.counter("st_lo", 1)
        q_scores = m.counter("q_scores", 2 * NW)
        maxed = m.counter("maxed", 2 * NW)
        maxT_mm = m.counter("maxT_mm", NW)
        maxT_sb = m.counter("maxT_sb", NW)
        k_scores = m.counter("k_scores", NW)
        exped = m.counter("exped", NW)
        pv_mm = m.counter("pv_mm", NW)
        recip = m.counter("recip", NW)
        o_norm = m.counter("o_norm", 2 * NW)
        oT_mm = m.counter("oT_mm", NW)
        oT_hi = m.counter("oT_hi", NW)
        oT_lo = m.counter("oT_lo", NW)
        gate_mm = m.counter("gate_mm", TT)
        y_mm = m.counter("y_mm", TT)
        gate_sb = m.counter("gate_sb", TT)
        gated = m.counter("gated", TT)
        mixed = m.counter("mixed", TT)
        x1_sb = m.counter("x1_sb", TT)
        x1_out = m.counter("x1_out", 16)
        block = ctx.enter_context(nc.Block())
        pvO = pv[:, 0:PAIRS * (2 * DH + 1)].rearrange("p (a d) -> p a d", a=PAIRS)
        steps = range(NW + 3)

        def by_window(ap):
            return ap.rearrange("p (n q) -> p n q", n=NW)

        def loop(eng, body):
            body(0, False)
            with eng.Fori(1, NB - 1) as b:
                body(b, False)
            body(NB - 1, True)

        @block.sync
        def _(sp):
            def load(b):
                sp.dma_start(x[:], din["x"][bass.ds(b, 1), :, :].rearrange("a (t p) d -> p (a t) d", p=P)
                             ).then_inc(x_in.sem, 16)
                row = scratch["mod"][bass.ds(b, 1), 0:2 * D].rearrange("a (i d) -> a i d", i=2)
                sp.dma_start(shsc[:], row.to_broadcast([P, 2, D])).then_inc(x_in.sem, 16)

            def body(b, last):
                sp.wait_ge(k_lo.sem, k_lo.at(b, 2))
                for j in range(4):
                    r = slice(32 * j, 32 * j + 32)
                    sp.dma_start(Kz[r, j, :, :, WIN:], Kt[r, :, :, :]).then_inc(k_spread.sem, 16)
                if not last:
                    sp.wait_ge(s_norm0.sem, s_norm0.at(b, 4))
                    sp.wait_ge(s_h.sem, s_h.at(b, 2))
                    load(b + 1)
                sp.wait_ge(s_h.sem, s_h.at(b, 2))
                sp.wait_ge(x1_sb.sem, x1_sb.at(b, 0))
                sp.dma_start(hres[:], h[:]).then_inc(h_kept.sem, 16)
                sp.wait_ge(x1_sb.sem, x1_sb.at(b, TT))
                sp.dma_start(scratch["x1"][bass.ds(b, 1), :, :].rearrange("a (t p) d -> p (a t) d", p=P),
                             x1[:]).then_inc(x1_out.sem, 16)

            load(0)
            loop(sp, body)
            sp.wait_ge(x1_out.sem, 16 * NB)

        @block.tensor
        def _(pe):
            def project(b):
                for k in range(KD):
                    if k == 0:
                        pe.wait_ge(s_norm1.sem, s_norm1.at(b, 4))
                    for t in range(TT):
                        last = pe.transpose(pj[:, k, t * P:(t + 1) * P], nrm[:, t, k * P:(k + 1) * P],
                                            w["identf"][:])
                    last.then_inc(xT_mm.sem, 1)
                pe.wait_ge(xT_lo.sem, xT_lo.at(b, 2))
                for c in range(4):
                    if c in (2, 3):
                        pe.wait_ge(q_lo.sem, q_lo.at(b, 2 * (c - 1)))
                    for k in range(KD):
                        last = hi_lo_products(pe, pj[:, c % 2, :], [a[:, k, c * P:(c + 1) * P] for a in w["qk"]],
                                              [a[:, k, WIN:] for a in (xTh, xTl)], k == 0, k == KD - 1)
                    last.then_inc((q_mm if c < 2 else k_mm).sem, 1)
                for u in range(4):
                    if u < 2:
                        pe.wait_ge(k_lo.sem, k_lo.at(b, u + 1))
                    else:
                        pe.wait_ge(v_sb.sem, v_sb.at(b, u - 1))
                    for i in range(2):
                        t0 = WIN * (2 * u + i)
                        for k in range(KD):
                            last = hi_lo_products(pe, pj[:, u % 2, i * D:(i + 1) * D],
                                                  [a[:, k, t0:t0 + P] for a in (xTh, xTl)],
                                                  [a[:, k, :] for a in w["v"]], k == 0, k == KD - 1)
                    last.then_inc(v_mm.sem, 1)
                pe.wait_ge(v_sb.sem, v_sb.at(b, 3))
                for k in range(KD):
                    last = hi_lo_products(pe, pj[:, 0, :], [a[:, k, :] for a in w["drive"]],
                                          [a[:, k, WIN:] for a in (xTh, xTl)], k == 0, k == KD - 1)
                last.then_inc(drive_mm.sem, 1)

            def scores_by_query(b, n):
                var = 1 if n == 0 else 0
                for c in range(2):
                    if n == 0:
                        pe.wait_ge(gated.sem, gated.at(b, 0))
                    else:
                        pe.wait_ge(maxed.sem, maxed.at(b, 2 * n - 1 + c))
                    pe.matmul(sc[:, c, :], w["twoI"][:], w["maskq"][:, var, :, :], start=True, stop=False)
                    for j in range(4):
                        last = pe.matmul(sc[:, c, j * P:(j + 1) * P],
                                         Qh[:, c, n, :, :].rearrange("p a q -> p (a q)"),
                                         Kz[:, j, 0, c, WIN * n:WIN * n + P], start=False, stop=(j == 3))
                    last.then_inc(q_scores.sem, 1)

            def scores_by_key(b, n):
                pe.wait_ge(maxT_sb.sem, maxT_sb.at(b, n + 1))
                if n > 0:
                    pe.wait_ge(exped.sem, exped.at(b, n))
                var = 1 if n == 0 else 0
                for c in range(2):
                    q = [a[:, c, n, :, :].rearrange("p a q -> p (a q)") for a in (Qh, Ql)]
                    for j in range(4):
                        out = sc[:, 2 + c, j * P:(j + 1) * P]
                        pe.matmul(out, w["select"][:, var, 4 * c + j, :], w["shift"][:, n % 2, :],
                                  start=True, stop=False)
                        last = hi_lo_products(pe, out, [Kz[:, j, i, c, WIN * n:WIN * n + P] for i in range(2)],
                                              q, False, True)
                last.then_inc(k_scores.sem, 1)

            def values(b, n):
                pe.wait_ge(exped.sem, exped.at(b, n + 1))
                if n > 0:
                    pe.wait_ge(o_norm.sem, o_norm.at(b, 2 * n))
                for i in range(PAIRS):
                    last = pe.matmul(pvO[:, i, :], prob[:, n % 2, i * P:(i + 1) * P], V[:, n, i, :],
                                     start=True, stop=True)
                last.then_inc(pv_mm.sem, 1)

            def out_tile(b, t):
                pe.wait_ge(oT_lo.sem, oT_lo.at(b, 2 * t + 2))
                if t == 0:
                    pe.wait_ge(st_lo.sem, st_lo.at(b, 1))
                tok = slice(t * P, (t + 1) * P)
                for k in range(KD):
                    hi_lo_products(pe, sc[:, t, 0:D], [a[:, k, WIN + t * P:WIN + (t + 1) * P] for a in (xTh, xTl)],
                                   [a[:, k, :] for a in w["g"]], k == 0, False)
                pe.matmul(sc[:, t, 0:D], w["ones3"][:], w["bg3"][:], start=False, stop=True)
                for par in range(2):
                    hi_lo_products(pe, sc[:, t, D:], [a[:, par, tok] for a in (oTh, oTl)],
                                   [a[:, par, :] for a in w["o"]], par == 0, False)
                hi_lo_products(pe, sc[:, t, D:], [sth[:, tok], stl[:, tok]], [a[:, 0, :] for a in w["nc"]],
                               False, False)
                pe.matmul(sc[:, t, D:], w["ones3"][:], w["bo3"][:], start=False, stop=True).then_inc(gate_mm.sem, 1)
                if t >= 2:
                    pe.wait_ge(mixed.sem, mixed.at(b, t - 1))
                else:
                    pe.wait_ge(oT_lo.sem, oT_lo.at(b, NW))
                hi_lo_products(pe, pj[:, (t + 1) % 2, 0:D], [sth[:, tok], stl[:, tok]],
                               [a[:, 0, :] for a in w["c"]], True, True).then_inc(y_mm.sem, 1)

            def body(b, last):
                project(b)
                for s in steps:
                    if s < NW:
                        if s == 0:
                            pe.wait_ge(k_spread.sem, k_spread.at(b, 64))
                        scores_by_query(b, s)
                    if 0 <= s - 1 < NW:
                        scores_by_key(b, s - 1)
                    if 0 <= s - 2 < NW:
                        if s == 2:
                            pe.wait_ge(v_sb.sem, v_sb.at(b, 4))
                        values(b, s - 2)
                    if s < NW:
                        pe.wait_ge(maxed.sem, maxed.at(b, 2 * s + 2))
                        pe.transpose(pm[:], mx[:, s % 2, :], w["identb"][:]).then_inc(maxT_mm.sem, 1)
                    if 0 <= s - 3 < NW:
                        n = s - 3
                        pe.wait_ge(o_norm.sem, o_norm.at(b, 2 * n + 2))
                        if n >= 2:
                            pe.wait_ge(oT_lo.sem, oT_lo.at(b, n - 1))
                        else:
                            pe.wait_ge(drive_sb.sem, drive_sb.at(b, 1))
                        pe.transpose(pj[:, n % 2, 0:P], on[:, n % 2, :, :], w["identf"][:]).then_inc(oT_mm.sem, 1)
                for t in range(TT):
                    out_tile(b, t)
                pe.wait_ge(mixed.sem, mixed.at(b, TT))

            loop(pe, body)

        @block.scalar
        def _(act):
            def body(b, last):
                for k in range(KD):
                    act.wait_ge(xT_mm.sem, xT_mm.at(b, k + 1))
                    if k == 0:
                        act.wait_ge(xT_lo.sem, xT_lo.at(b, 0))
                    act.activation(xTf[:, k, :], pj[:, k, :], ACT.Identity, bias=w["b1"][:, k:k + 1],
                                   scale=w["g1"][:, k:k + 1]).then_inc(xT_f.sem, 1)
                for c in range(2):
                    act.wait_ge(q_mm.sem, q_mm.at(b, c + 1))
                    for par in range(2):
                        act.mul(Qh[:, c, :, par, :], by_window(pj[:, c, :]), w["parity"][:, par:par + 1]).then_inc(q_hi.sem, 1)
                for c in range(2):
                    act.wait_ge(k_mm.sem, k_mm.at(b, c + 1))
                    act.copy(Kt[:, 0, c, :], pj[:, c, :]).then_inc(k_hi.sem, 1)
                for u in range(4):
                    act.wait_ge(v_mm.sem, v_mm.at(b, u + 1))
                    act.copy(V[:, 2 * u:2 * u + 2, :, 0:2 * DH],
                             pj[:, u % 2, :].rearrange("p (n a d) -> p n a d", n=2, a=PAIRS)
                             ).then_inc(v_sb.sem, 1)
                act.wait_ge(drive_mm.sem, drive_mm.at(b, 1))
                act.wait_ge(scanned.sem, scanned.at(b, 0))
                act.activation(drv[:], pj[:, 0, :], ACT.Identity, bias=w["bu"][:, 0:1]).then_inc(drive_sb.sem, 1)
                for s in steps:
                    if 0 <= s - 1 < NW:
                        n = s - 1
                        act.wait_ge(k_scores.sem, k_scores.at(b, n + 1))
                        act.activation(prob[:, n % 2, :].rearrange("p (c j) -> p c j", c=2), sc[:, 2:4, :],
                                       ACT.Exp, scale=SCALE).then_inc(exped.sem, 1)
                    if 0 <= s - 3 < NW:
                        n = s - 3
                        act.wait_ge(oT_mm.sem, oT_mm.at(b, n + 1))
                        act.copy(oTh[:, :, WIN * n:WIN * n + WIN],
                                 pj[:, n % 2, 0:P].rearrange("p (a q) -> p a q", a=2)).then_inc(oT_hi.sem, 1)
                for t in range(TT):
                    act.wait_ge(gate_mm.sem, gate_mm.at(b, t + 1))
                    if t == 0:
                        act.wait_ge(x1_sb.sem, x1_sb.at(b, 0))
                    act.activation(mix[:, t, :], sc[:, t, 0:D], ACT.Tanh, scale=0.5).then_inc(gate_sb.sem, 1)

            loop(act, body)

        def moments(dve, b, src, half):
            for t in range(TT):
                dve.bn_stats(stats[:, t, :], src[:, t, :]).then_inc(s_stats.sem, 1)

        def aggregate(dve, b, half):
            wait_alone(dve, s_stats.sem, s_stats.at(b, 4 * half + 4), dve_passed)
            for t in range(TT):
                dve.bn_aggr(mv[:, t, :], stats[:, t, :]).then_inc(s_aggr.sem, 1)
            dve.wait_ge(s_aggr.sem, s_aggr.at(b, 4 * half + 4))
            seed_inverse_root(dve, s_seed, b, SEED * half, mv[:, :, 1], ve[:], rs[:])

        def normalize(dve, b, src, half, done):
            dve.wait_ge(s_rstd.sem, s_rstd.at(b, NEWTON * (half + 1)))
            for t in range(TT):
                dve.tensor_scalar(nrm[:, t, :], src[:, t, :], mv[:, t, 0:1], rs[:, t:t + 1], ALU.subtract,
                                  ALU.mult).then_inc(done.sem, 1)

        def layer_norms(dve, b, part):
            if part == 0:
                dve.wait_ge(x_in.sem, x_in.at(b, 32))
                moments(dve, b, x, 0)
            if part == 1:
                aggregate(dve, b, 0)
            if part == 2:
                dve.wait_ge(xT_mm.sem, xT_mm.at(b, 0))
                normalize(dve, b, x, 0, s_norm0)
            if part == 6:
                dve.wait_ge(s_h.sem, s_h.at(b, 2))
                moments(dve, b, h, 1)
            if part == 7:
                aggregate(dve, b, 1)
            if part == 8:
                normalize(dve, b, h, 1, s_norm1)

        @block.vector
        def _(dve):
            def body(b, last):
                for k in range(KD):
                    dve.wait_ge(xT_f.sem, xT_f.at(b, k + 1))
                    dve.tensor_copy(xTh[:, k, WIN:], xTf[:, k, :]).then_inc(xT_hi.sem, 1)
                for c in range(2):
                    dve.wait_ge(q_hi.sem, q_hi.at(b, 2 * c + 2))
                    for par in range(2):
                        dve.scalar_tensor_tensor(out=Ql[:, c, :, par, :], in0=by_window(pj[:, c, :]),
                                                 scalar=w["parity"][:, par:par + 1], in1=Qh[:, c, :, par, :],
                                                 op0=ALU.mult, op1=ALU.subtract).then_inc(q_lo.sem, 1)
                for c in range(2):
                    dve.wait_ge(k_hi.sem, k_hi.at(b, c + 1))
                    dve.tensor_tensor(Kt[:, 1, c, :], pj[:, c, :], Kt[:, 0, c, :], ALU.subtract
                                      ).then_inc(k_lo.sem, 1)
                for s in steps:
                    if s < NW:
                        for c in range(2):
                            dve.wait_ge(q_scores.sem, q_scores.at(b, 2 * s + c + 1))
                            dve.tensor_reduce(mx[:, s % 2, WIN + 4 * c:WIN + 4 * c + 4],
                                              sc[:, c, :].rearrange("p (j k) -> p j k", j=4),
                                              AX.X, ALU.max).then_inc(maxed.sem, 1)
                    if s == 1:
                        dve.wait_ge(drive_sb.sem, drive_sb.at(b, 1))
                        dve.wait_ge(st_lo.sem, st_lo.at(b, 0))
                        dve.tensor_tensor_scan(st[:], w["A"][:, 0:1].to_broadcast([P, L]), drv[:], 0.0, ALU.mult,
                                               ALU.add).then_inc(scanned.sem, 1)
                        dve.wait_ge(scanned.sem, scanned.at(b, 1))
                        dve.tensor_copy(sth[:], st[:]).then_inc(st_hi.sem, 1)
                    if not last:
                        layer_norms(dve, b + 1, s)
                    if 0 <= s - 2 < NW:
                        n = s - 2
                        dve.wait_ge(pv_mm.sem, pv_mm.at(b, n + 1))
                        dve.reciprocal(rden[:, n % 2, :], pvO[:, :, 2 * DH]).then_inc(recip.sem, 1)
                        dve.wait_ge(recip.sem, recip.at(b, n + 1))
                        for par in range(2):
                            r = slice(WIN * par, WIN * par + WIN)
                            dve.tensor_tensor(on[r, n % 2, :, :], pvO[r, :, DH * par:DH * par + DH],
                                              rden[r, n % 2, :].unsqueeze(2).to_broadcast([WIN, PAIRS, DH]),
                                              ALU.mult).then_inc(o_norm.sem, 1)
                    if s < NW:
                        dve.wait_ge(maxT_mm.sem, maxT_mm.at(b, s + 1))
                        dve.tensor_copy(w["shift"][WIN:WIN + PAIRS, s % 2, :], pm[WIN:WIN + PAIRS, :]).then_inc(maxT_sb.sem, 1)
                    if 0 <= s - 3 < NW:
                        n = s - 3
                        dve.wait_ge(oT_hi.sem, oT_hi.at(b, n + 1))
                        dve.tensor_tensor(oTl[:, :, WIN * n:WIN * n + WIN],
                                          pj[:, n % 2, 0:P].rearrange("p (a q) -> p a q", a=2),
                                          oTh[:, :, WIN * n:WIN * n + WIN], ALU.subtract).then_inc(oT_lo.sem, 1)
                for t in range(TT):
                    dve.wait_ge(gate_sb.sem, gate_sb.at(b, t + 1))
                    dve.scalar_tensor_tensor(out=mix[:, t, :], in0=mix[:, t, :], scalar=1.0, in1=sc[:, t, D:],
                                             op0=ALU.add, op1=ALU.mult).then_inc(gated.sem, 1)
                    dve.wait_ge(gated.sem, gated.at(b, t + 1))
                    dve.wait_ge(y_mm.sem, y_mm.at(b, t + 1))
                    dve.scalar_tensor_tensor(out=mix[:, t, :], in0=mix[:, t, :], scalar=0.5,
                                             in1=pj[:, (t + 1) % 2, 0:D], op0=ALU.mult, op1=ALU.add
                                             ).then_inc(mixed.sem, 1)

            for part in range(9):
                layer_norms(dve, 0, part)
            loop(dve, body)

        @block.gpsimd
        def _(pool):
            def inverse_deviation(b, half):
                pool.wait_ge(s_seed.sem, s_seed.at(b, SEED * (half + 1)))
                refine_inverse_root(pool, s_rstd, b, NEWTON * half, ve[:], rs[:], nt[:], pool_passed)

            def modulate(b):
                inverse_deviation(b, 0)
                pool.wait_ge(s_norm0.sem, s_norm0.at(b, 4))
                pool.wait_ge(h_kept.sem, h_kept.at(b, 0))
                pool.tensor_tensor(h[:], nrm[:], shsc[:, 1:2, :].to_broadcast([P, TT, D]), ALU.mult
                                   ).then_inc(s_h.sem, 1)
                pool.wait_ge(s_h.sem, s_h.at(b, 1))
                pool.tensor_tensor(h[:], h[:], shsc[:, 0:1, :].to_broadcast([P, TT, D]), ALU.add
                                   ).then_inc(s_h.sem, 1)
                inverse_deviation(b, 1)

            def body(b, last):
                for k in range(KD):
                    pool.wait_ge(xT_hi.sem, xT_hi.at(b, k + 1))
                    pool.tensor_tensor(xTl[:, k, WIN:], xTf[:, k, :], xTh[:, k, WIN:], ALU.subtract
                                       ).then_inc(xT_lo.sem, 1)
                pool.wait_ge(st_hi.sem, st_hi.at(b, 1))
                pool.tensor_tensor(stl[:], st[:], sth[:], ALU.subtract).then_inc(st_lo.sem, 1)
                if not last:
                    modulate(b + 1)
                pool.wait_ge(h_kept.sem, h_kept.at(b, 16))
                pool.wait_ge(x1_out.sem, x1_out.at(b, 0))
                for t in range(TT):
                    pool.wait_ge(mixed.sem, mixed.at(b, t + 1))
                    pool.tensor_tensor(x1[:, t, :], mix[:, t, :], hres[:, t, :], ALU.add).then_inc(x1_sb.sem, 1)

            modulate(0)
            loop(pool, body)



ROUTE = 19


def mlp(nc, din, w, scratch, NB, keep, capacity):
    with ExitStack() as ctx:
        m = Memory(nc, ctx, "mlp_")
        xa = m.sb("xa", [P, TT, D])
        xb = m.sb("xb", [P, TT, D])
        x = m.sb("x", [P, TT, D])
        ga = m.sb("ga", [P, 1, D])
        shsc = m.sb("shsc", [P, 2, D])
        nrm = m.sb("nrm", [P, TT, D])
        stats = m.sb("stats", [P, TT, 6])
        mv = m.sb("mv", [P, TT, 2])
        ve, rs, nt = (m.sb(n, [P, TT]) for n in ("ve", "rs", "nt"))
        stats3 = m.sb("stats3", [P, TT, 6])
        mv3 = m.sb("mv3", [P, TT, 2])
        ve3, rs3, nt3 = (m.sb(n, [P, TT]) for n in ("ve3", "rs3", "nt3"))
        xTf = m.sb("xTf", [P, KD, L])
        xT = [m.sb(n, [P, KD, L], F16) for n in ("xTh", "xTl")]
        hid = m.sb("hid", [P, 2, L])
        hd = [m.sb(n, [P, FMC, L], F16) for n in ("hidh", "hidl")]
        x2 = m.sb("x2", [P, TT, D])
        h2 = m.sb("h2", [P, TT, D])
        rows = m.sb("rows", [P, TT, 2, D], F16)
        hT = m.sb("hT", [P, TT, 4, P], F16)
        lg = m.sb("lg", [P, TT, E])
        srt = m.sb("srt", [P, TT, 8])
        ix = m.sb("ix", [P, TT, 8], U32)
        ixf = m.sb("ixf", [P, TT * 2])
        oh = m.sb("oh", [P, TT * 2, E])
        mem = m.sb("mem", [P, TT, E], BF16)
        pos = m.sb("pos", [P, TT, E])
        picked = m.sb("picked", [P, TT * 2, E])
        slotf = m.sb("slotf", [P, TT * 2])
        slot = m.sb("slot", [P, TT * 2], I32)
        iota8 = m.sb("iota8", [P, E])
        pj = m.ps("pj", [P, 2, 512])
        po = m.ps("po", [P, 2, 512])
        pt = m.ps("pt", [P, 2, 1024], F16)
        pg = m.ps("pg", [P, 512])
        pp = m.ps("pp", [P, 512])
        base = keep["base"]

        xa_in = m.counter("xa_in", 16)
        xb_in = m.counter("xb_in", 48)
        sh_in = m.counter("sh_in", 16)
        dve_passed, pool_passed = m.counter("dve_passed"), m.counter("pool_passed")
        s_stats, s_aggr = m.counter("s_stats", 4), m.counter("s_aggr", 4)
        s_seed, s_rstd = m.counter("s_seed", SEED), m.counter("s_rstd", NEWTON)
        s_norm = m.counter("s_norm", 4)
        t_stats, t_aggr = m.counter("t_stats", 4), m.counter("t_aggr", 4)
        t_seed, t_rstd = m.counter("t_seed", SEED), m.counter("t_rstd", NEWTON)
        t_norm = m.counter("t_norm", 4)
        xT_mm, xT_f = m.counter("xT_mm", 2), m.counter("xT_f", 2)
        xT_hi, xT_lo = m.counter("xT_hi", 2), m.counter("xT_lo", 2)
        hid_mm, hid_f = m.counter("hid_mm", FMC), m.counter("hid_f", FMC)
        hid_hi, hid_lo = m.counter("hid_hi", FMC), m.counter("hid_lo", FMC)
        out_mm = m.counter("out_mm", TT)
        out_sb = m.counter("out_sb", TT)
        x2_sb = m.counter("x2_sb", 2)
        x2_out = m.counter("x2_out", 16)
        s_h2 = m.counter("s_h2", 2)
        row_hi, row_lo = m.counter("row_hi", 1), m.counter("row_lo", 1)
        hT_mm, hT_sb = m.counter("hT_mm", 2), m.counter("hT_sb", 2)
        gate_mm = m.counter("gate_mm", 1)
        prefix_mm = m.counter("prefix_mm", 1)
        route = m.counter("route", ROUTE)
        sent = m.counter("sent", 16 * 2 * TT)
        ready = m.counter("ready", 1)
        block = ctx.enter_context(nc.Block())

        def loop(eng, body):
            body(0, True, False)
            body(1, False, False)
            with eng.Fori(2, NB - 1) as b:
                body(b, False, False)
            body(NB - 1, False, True)

        def rows_of(ap, b):
            return ap[bass.ds(b, 1), :, :].rearrange("a (t p) d -> p (a t) d", p=P)

        @block.sync
        def _(sp):
            def load_x1(b):
                sp.dma_start(xa[:], rows_of(scratch["x1"], b)).then_inc(xa_in.sem, 16)

            def body(b, first, last):
                sp.wait_ge(x2_sb.sem, x2_sb.at(b, 0))
                sp.dma_start(xb[:], rows_of(scratch["x1"], b)).then_inc(xb_in.sem, 16)
                sp.dma_start(x[:], rows_of(din["x"], b)).then_inc(xb_in.sem, 16)
                sp.dma_start(ga[:], scratch["mod"][bass.ds(b, 1), 2 * D:3 * D].rearrange("a (i d) -> a i d", i=1)
                             .to_broadcast([P, 1, D])).then_inc(xb_in.sem, 16)
                if not last:
                    sp.wait_ge(s_norm.sem, s_norm.at(b, 4))
                    load_x1(b + 1)
                sp.wait_ge(s_h2.sem, s_h2.at(b, 0))
                sp.dma_start(shsc[:], scratch["mod"][bass.ds(b, 1), 3 * D:5 * D]
                             .rearrange("a (i d) -> a i d", i=2).to_broadcast([P, 2, D])).then_inc(sh_in.sem, 16)
                sp.wait_ge(x2_sb.sem, x2_sb.at(b, 2))
                sp.dma_start(rows_of(scratch["x2"], b), x2[:]).then_inc(x2_out.sem, 16)

            load_x1(0)
            loop(sp, body)
            sp.wait_ge(x2_out.sem, 16 * NB)

        @block.tensor
        def _(pe):
            def transpose_x(b):
                for k in range(KD):
                    if k == 0:
                        pe.wait_ge(s_norm.sem, s_norm.at(b, 4))
                        pe.wait_ge(hid_f.sem, hid_f.at(b, 0))
                    for t in range(TT):
                        last = pe.transpose(pj[:, k, t * P:(t + 1) * P], nrm[:, t, k * P:(k + 1) * P],
                                            w["identf"][:])
                    last.then_inc(xT_mm.sem, 1)
                pe.wait_ge(xT_lo.sem, xT_lo.at(b, 2))

            def hidden(b, c):
                if c >= 2:
                    pe.wait_ge(hid_f.sem, hid_f.at(b, c - 1))
                for k in range(KD):
                    last = hi_lo_products(pe, pj[:, c % 2, :], [a[:, k, c * P:(c + 1) * P] for a in w["w1"]],
                                          [a[:, k, :] for a in xT], k == 0, k == KD - 1)
                last.then_inc(hid_mm.sem, 1)

            def project(b, t):
                if t == 0:
                    pe.wait_ge(hid_lo.sem, hid_lo.at(b, FMC))
                if t >= 2:
                    pe.wait_ge(out_sb.sem, out_sb.at(b, t - 1))
                else:
                    pe.wait_ge(out_sb.sem, out_sb.at(b, 0))
                for c in range(FMC):
                    hi_lo_products(pe, po[:, t % 2, 0:D], [a[:, c, t * P:(t + 1) * P] for a in hd],
                                   [a[:, c, :] for a in w["w2"]], c == 0, False)
                pe.matmul(po[:, t % 2, 0:D], w["ones3"][:], w["b23"][:], start=False, stop=True
                          ).then_inc(out_mm.sem, 1)

            def transpose_rows(a):
                pe.wait_ge(row_lo.sem, row_lo.at(a, 1))
                for u in range(2):
                    for t in (2 * u, 2 * u + 1):
                        for i in range(2):
                            for k in range(KD):
                                at = ((t % 2) * 4 + i * 2 + k) * P
                                last = pe.transpose(pt[:, u, at:at + P], rows[:, t, i, k * P:(k + 1) * P],
                                                    w["identh"][:])
                    last.then_inc(hT_mm.sem, 1)

            def gate(a):
                pe.wait_ge(hT_sb.sem, hT_sb.at(a, 2))
                for t in range(TT):
                    for k in range(KD):
                        last = hi_lo_products(pe, pg[:, t * E:(t + 1) * E], [hT[:, t, i * 2 + k, :] for i in range(2)],
                                              [g[:, k, :] for g in w["gate"]], k == 0, k == KD - 1)
                last.then_inc(gate_mm.sem, 1)

            def prefix(a):
                pe.wait_ge(route.sem, route.at(a, 12))
                flat = mem[:].rearrange("p t e -> p (t e)")
                pe.matmul(pp[:, 0:TT * E], w["before"][:], flat, start=True, stop=False)
                for t in range(1, TT):
                    pe.matmul(pp[:, t * E:TT * E], w["ones"][:], flat[:, 0:(TT - t) * E], start=False,
                              stop=(t == TT - 1))
                for t in range(TT):
                    last = pe.matmul(pp[:, TT * E:TT * E + E], w["ones"][:], mem[:, t, :], start=(t == 0),
                                     stop=(t == TT - 1))
                last.then_inc(prefix_mm.sem, 1)

            def body(b, first, last):
                transpose_x(b)
                for c in range(FMC):
                    hidden(b, c)
                    if not first and c == 4:
                        transpose_rows(b - 1)
                    if not first and c == 5:
                        gate(b - 1)
                for t in range(TT):
                    project(b, t)
                    if not first and t == 0:
                        prefix(b - 1)

            loop(pe, body)
            transpose_rows(NB - 1)
            gate(NB - 1)
            prefix(NB - 1)

        @block.scalar
        def _(act):
            def copy_rows(a):
                for u in range(2):
                    act.wait_ge(hT_mm.sem, hT_mm.at(a, u + 1))
                    act.copy(hT[:, 2 * u:2 * u + 2, :, :].rearrange("p t i q -> p (t i q)"), pt[:, u, :]
                             ).then_inc(hT_sb.sem, 1)

            def body(b, first, last):
                for k in range(KD):
                    act.wait_ge(xT_mm.sem, xT_mm.at(b, k + 1))
                    act.activation(xTf[:, k, :], pj[:, k, :], ACT.Identity, bias=w["b2"][:, k:k + 1],
                                   scale=w["g2"][:, k:k + 1]).then_inc(xT_f.sem, 1)
                for c in range(FMC):
                    act.wait_ge(hid_mm.sem, hid_mm.at(b, c + 1))
                    if c >= 2:
                        act.wait_ge(hid_lo.sem, hid_lo.at(b, c - 1))
                    act.activation(hid[:, c % 2, :], pj[:, c % 2, :], ACT.Gelu, bias=w["mb1"][:, c:c + 1]
                                   ).then_inc(hid_f.sem, 1)
                    if not first and c == 4:
                        copy_rows(b - 1)

            loop(act, body)
            copy_rows(NB - 1)

        def moments(dve, b, src, st, out, sig_st, sig_ag, seed, v, y):
            for t in range(TT):
                dve.bn_stats(st[:, t, :], src[:, t, :]).then_inc(sig_st.sem, 1)
            wait_alone(dve, sig_st.sem, sig_st.at(b, 4), dve_passed)
            for t in range(TT):
                dve.bn_aggr(out[:, t, :], st[:, t, :]).then_inc(sig_ag.sem, 1)
            dve.wait_ge(sig_ag.sem, sig_ag.at(b, 4))
            seed_inverse_root(dve, seed, b, 0, out[:, :, 1], v[:], y[:])

        @block.vector
        def _(dve):
            def norm_x1(b):
                dve.wait_ge(xa_in.sem, xa_in.at(b, 16))
                moments(dve, b, xa, stats, mv, s_stats, s_aggr, s_seed, ve, rs)
                dve.wait_ge(s_rstd.sem, s_rstd.at(b, NEWTON))
                dve.wait_ge(xT_mm.sem, xT_mm.at(b, 0))
                for t in range(TT):
                    dve.tensor_scalar(nrm[:, t, :], xa[:, t, :], mv[:, t, 0:1], rs[:, t:t + 1], ALU.subtract,
                                      ALU.mult).then_inc(s_norm.sem, 1)

            def stats_x2(a):
                dve.wait_ge(x2_sb.sem, x2_sb.at(a, 2))
                moments(dve, a, x2, stats3, mv3, t_stats, t_aggr, t_seed, ve3, rs3)

            def norm_x2(a):
                dve.wait_ge(t_rstd.sem, t_rstd.at(a, NEWTON))
                for t in range(TT):
                    dve.tensor_scalar(h2[:, t, :], x2[:, t, :], mv3[:, t, 0:1], rs3[:, t:t + 1], ALU.subtract,
                                      ALU.mult).then_inc(t_norm.sem, 1)

            def split_rows(a):
                dve.wait_ge(s_h2.sem, s_h2.at(a, 2))
                dve.wait_ge(sent.sem, sent.at(a, 0))
                dve.tensor_copy(rows[:, :, 0, :], h2[:]).then_inc(row_hi.sem, 1)

            def choose(a):
                n = 0

                def step(ins, wait=True):
                    nonlocal n
                    ins.then_inc(route.sem, 1)
                    n += 1
                    if wait:
                        wait_alone(dve, route.sem, route.at(a, n), dve_passed)

                dve.wait_ge(gate_mm.sem, gate_mm.at(a, 1))
                step(dve.tensor_copy(lg[:].rearrange("p t e -> p (t e)"), pg[:, 0:TT * E]))
                for t in range(TT):
                    step(dve.max(srt[:, t, :], lg[:, t, :]), t == TT - 1)
                for t in range(TT):
                    step(dve.max_index(ix[:, t, :], srt[:, t, :], lg[:, t, :]), t == TT - 1)
                step(dve.tensor_copy(ixf[:].rearrange("p (t k) -> p t k", k=2), ix[:, :, 0:2]))
                step(dve.tensor_tensor(oh[:], iota8[:].unsqueeze(1).to_broadcast([P, 2 * TT, E]),
                                       ixf[:].unsqueeze(2).to_broadcast([P, 2 * TT, E]), ALU.is_equal))
                both = oh[:].rearrange("p (t k) e -> p t k e", k=2)
                step(dve.tensor_tensor(mem[:], both[:, :, 0, :], both[:, :, 1, :], ALU.add))
                step(dve.tensor_copy(keep["top"][:, bass.ds(a * TT, TT), :], srt[:, :, 0:2]), False)
                return n

            def place(a):
                n = 13
                dve.wait_ge(prefix_mm.sem, prefix_mm.at(a, 1))
                both = oh[:].rearrange("p (t k) e -> p t k e", k=2)
                for ins in (
                    lambda: dve.tensor_tensor(pos[:], pp[:, 0:TT * E].rearrange("p (t e) -> p t e", e=E),
                                              base[:].unsqueeze(1).to_broadcast([P, TT, E]), ALU.add),
                    lambda: dve.tensor_tensor(base[:], base[:], pp[:, TT * E:TT * E + E], ALU.add),
                    lambda: dve.tensor_tensor(picked[:].rearrange("p (t k) e -> p t k e", k=2), both,
                                              pos[:].unsqueeze(2).to_broadcast([P, TT, 2, E]), ALU.mult),
                    lambda: dve.tensor_reduce(slotf[:], picked[:], AX.X, ALU.add),
                    lambda: dve.tensor_copy(slot[:], slotf[:]),
                    lambda: dve.tensor_copy(keep["slots"][:, bass.ds(a * 2 * TT, 2 * TT)], slotf[:]),
                ):
                    ins().then_inc(route.sem, 1)
                    n += 1
                    dve.wait_ge(route.sem, route.at(a, n))

            def body(b, first, last):
                for k in range(KD):
                    dve.wait_ge(xT_f.sem, xT_f.at(b, k + 1))
                    dve.tensor_copy(xT[0][:, k, :], xTf[:, k, :]).then_inc(xT_hi.sem, 1)
                for c in range(FMC):
                    if not first:
                        if c == 0:
                            stats_x2(b - 1)
                        if c == 2:
                            norm_x2(b - 1)
                        if c == 4:
                            split_rows(b - 1)
                        if c == 7:
                            choose(b - 1)
                    dve.wait_ge(hid_f.sem, hid_f.at(b, c + 1))
                    dve.tensor_copy(hd[0][:, c, :], hid[:, c % 2, :]).then_inc(hid_hi.sem, 1)
                if not last:
                    norm_x1(b + 1)
                for t in range(TT):
                    if t == 0:
                        dve.wait_ge(xb_in.sem, xb_in.at(b, 48))
                    dve.wait_ge(out_mm.sem, out_mm.at(b, t + 1))
                    dve.tensor_tensor(xb[:, t, :], po[:, t % 2, 0:D], xb[:, t, :], ALU.add).then_inc(out_sb.sem, 1)
                    if not first and t == 1:
                        place(b - 1)

            dve.wait_ge(ready.sem, 2)
            norm_x1(0)
            loop(dve, body)
            a = NB - 1
            stats_x2(a)
            norm_x2(a)
            split_rows(a)
            choose(a)
            place(a)

        @block.gpsimd
        def _(pool):
            def modulate(a):
                pool.wait_ge(t_norm.sem, t_norm.at(a, 4))
                pool.wait_ge(sh_in.sem, sh_in.at(a, 16))
                for n, (i, op) in enumerate(((1, ALU.mult), (0, ALU.add))):
                    pool.tensor_tensor(h2[:], h2[:], shsc[:, i:i + 1, :].to_broadcast([P, TT, D]), op
                                       ).then_inc(s_h2.sem, 1)
                    pool.wait_ge(s_h2.sem, s_h2.at(a, n + 1))

            def low_rows(a):
                pool.wait_ge(row_hi.sem, row_hi.at(a, 1))
                pool.tensor_tensor(rows[:, :, 1, :], h2[:], rows[:, :, 0, :], ALU.subtract).then_inc(row_lo.sem, 1)

            def send(a):
                pool.wait_ge(route.sem, route.at(a, 18))
                wait_alone(pool, row_lo.sem, row_lo.at(a, 1), pool_passed)
                for t in range(TT):
                    for k in range(2):
                        pool.indirect_dma_start(
                            out=scratch["queue"], out_offset=bass.IndirectOffsetOnAxis(
                                ap=slot[:, 2 * t + k:2 * t + k + 1], axis=0),
                            in_=rows[:, t, :, :].rearrange("p i d -> p (i d)"), in_offset=None
                        ).then_inc(sent.sem, 16)

            def refine(b, sig, seed, v, y, a):
                pool.wait_ge(seed.sem, seed.at(b, SEED))
                refine_inverse_root(pool, sig, b, 0, v[:], y[:], a[:], pool_passed)

            def body(b, first, last):
                for k in range(KD):
                    pool.wait_ge(xT_hi.sem, xT_hi.at(b, k + 1))
                    pool.tensor_tensor(xT[1][:, k, :], xTf[:, k, :], xT[0][:, k, :], ALU.subtract
                                       ).then_inc(xT_lo.sem, 1)
                for c in range(FMC):
                    if not first:
                        if c == 0:
                            refine(b - 1, t_rstd, t_seed, ve3, rs3, nt3)
                        if c == 2:
                            modulate(b - 1)
                        if c == 4:
                            low_rows(b - 1)
                    pool.wait_ge(hid_hi.sem, hid_hi.at(b, c + 1))
                    pool.tensor_tensor(hd[1][:, c, :], hid[:, c % 2, :], hd[0][:, c, :], ALU.subtract
                                       ).then_inc(hid_lo.sem, 1)
                if not last:
                    refine(b + 1, s_rstd, s_seed, ve, rs, nt)
                if not first:
                    send(b - 1)
                pool.wait_ge(out_sb.sem, out_sb.at(b, TT))
                pool.wait_ge(x2_out.sem, x2_out.at(b, 0))
                pool.tensor_tensor(xb[:], xb[:], ga[:].to_broadcast([P, TT, D]), ALU.mult).then_inc(x2_sb.sem, 1)
                pool.wait_ge(x2_sb.sem, x2_sb.at(b, 1))
                pool.tensor_tensor(x2[:], xb[:], x[:], ALU.add).then_inc(x2_sb.sem, 1)

            pool.iota(iota8[:], pattern=[[1, E]], base=0, channel_multiplier=0,
                      allow_small_or_imprecise_dtypes=True).then_inc(ready.sem, 1)
            pool.iota(base[:], pattern=[[capacity, E]], base=0, channel_multiplier=0,
                      allow_small_or_imprecise_dtypes=True).then_inc(ready.sem, 1)
            refine(0, s_rstd, s_seed, ve, rs, nt)
            loop(pool, body)
            a = NB - 1
            refine(a, t_rstd, t_seed, ve3, rs3, nt3)
            modulate(a)
            low_rows(a)
            send(a)
            pool.wait_ge(sent.sem, 16 * 2 * TT * NB)



def plan(nc, keep, scratch, capacity, n_tiles):
    with ExitStack() as ctx:
        m = Memory(nc, ctx, "plan_")
        row = lambda name, n, dt=F32: m.sb(name, [1, n], dt)
        cnt, whole, cum, ones, move, step = (m.sb(n, [P, E]) for n in ("cnt", "whole", "cum", "ones", "move", "step"))
        cnti = m.sb("cnti", [P, E], I32)
        slots = keep["slots"]
        moved = m.sb("moved", list(slots.shape))
        extra = m.sb("extra", list(slots.shape))
        ends = row("ends", E, I32)
        top = row("top", 1)
        tile, ex, before, first = (row(n, n_tiles) for n in ("tile", "ex", "before", "first"))
        ge = m.sb("ge", [1, n_tiles, E])
        gn = m.sb("gn", [1, n_tiles, E])
        start = m.sb("start", [P, E])
        zeros = m.sb("zeros", [P, ROWS // P * 2 * D], F16)
        made = m.counter("made")
        planned = m.counter("planned")
        padded = m.counter("padded")
        block = ctx.enter_context(nc.Block())

        @block.gpsimd
        def _(pool):
            pool.iota(start[:], pattern=[[capacity, E]], base=0, channel_multiplier=0,
                      allow_small_or_imprecise_dtypes=True).then_inc(made.sem, 1)
            pool.iota(tile[:], pattern=[[1, n_tiles]], base=0, channel_multiplier=0,
                      allow_small_or_imprecise_dtypes=True).then_inc(made.sem, 1)
            pool.memset(ones[:], 1.0).then_inc(made.sem, 1)
            pool.memset(zeros[:], 0.0).then_inc(made.sem, 1)

        @block.vector
        def _(dve):
            per_tile = lambda ap: ap[:].unsqueeze(2).to_broadcast([1, n_tiles, E])
            per_expert = lambda ap: ap[0:1, :].unsqueeze(1).to_broadcast([1, n_tiles, E])
            base = keep["base"]
            dve.wait_ge(made.sem, 4)
            for n, ins in enumerate((
                lambda: dve.tensor_copy(ends[:], base[0:1, :]),
                lambda: dve.tensor_tensor(cnt[:], base[:], start[:], ALU.subtract),
                lambda: dve.tensor_scalar(cnti[:], cnt[:], float(ROWS - 1), None, ALU.add),
                lambda: dve.tensor_scalar(cnti[:], cnti[:], ROWS.bit_length() - 1, None, ALU.logical_shift_right),
                lambda: dve.tensor_copy(whole[:], cnti[:]),
                lambda: dve.tensor_tensor_scan(cum[:], ones[:], whole[:], 0.0, ALU.mult, ALU.add),
                lambda: dve.tensor_scalar(top[:], cum[0:1, E - 1:E], -1.0, None, ALU.add),
                lambda: dve.tensor_scalar(tile[:], tile[:], top[:, 0:1], None, ALU.min),
                lambda: dve.tensor_tensor(ge[:], per_tile(tile), per_expert(cum), ALU.is_ge),
                lambda: dve.tensor_reduce(ex[:], ge[:], AX.X, ALU.add),
                lambda: dve.tensor_tensor(gn[:], ge[:], per_expert(whole), ALU.mult),
                lambda: dve.tensor_reduce(before[:], gn[:], AX.X, ALU.add),
                lambda: dve.tensor_tensor(first[:], tile[:], before[:], ALU.subtract),
                lambda: dve.tensor_scalar(first[:], first[:], float(ROWS), None, ALU.mult),
                lambda: dve.scalar_tensor_tensor(out=first[:], in0=ex[:], scalar=float(capacity), in1=first[:],
                                                 op0=ALU.mult, op1=ALU.add),
                lambda: dve.tensor_copy(keep["tiles"][:, 0, :], ex[:]),
                lambda: dve.tensor_copy(keep["tiles"][:, 1, :], first[:]),
                lambda: dve.tensor_tensor(move[:], cum[:], whole[:], ALU.subtract),
                lambda: dve.scalar_tensor_tensor(out=move[:], in0=move[:], scalar=float(ROWS), in1=start[:],
                                                 op0=ALU.mult, op1=ALU.subtract),
                lambda: dve.tensor_tensor(step[:, 1:E], move[:, 1:E], move[:, 0:E - 1], ALU.subtract),
                lambda: dve.tensor_copy(moved[:], slots[:]),
                *(lambda e=e, half=half: (
                    dve.tensor_scalar(extra[:], slots[:], float(e * capacity), step[:, e:e + 1], ALU.is_ge, ALU.mult)
                    if half == 0 else dve.tensor_tensor(moved[:], moved[:], extra[:], ALU.add))
                  for e in range(1, E) for half in range(2)),
                lambda: dve.tensor_copy(keep["rows"][:], moved[:]),
            )):
                ins().then_inc(planned.sem, 1)
                dve.wait_ge(planned.sem, n + 1)

        @block.sync
        def _(sp):
            sp.wait_ge(made.sem, 4)
            sp.wait_ge(planned.sem, 1)
            for e in range(E):
                end = sp.value_load(ends[0:1, e:e + 1], min_val=e * capacity, max_val=(e + 1) * capacity - ROWS)
                sp.dma_start(scratch["queue"][bass.ds(end, ROWS), :].rearrange("(r p) d -> p r d", p=P),
                             zeros[:].rearrange("p (r d) -> p r d", r=ROWS // P)).then_inc(padded.sem, 16)
            sp.wait_ge(padded.sem, 16 * E)


def expert_weights(nc, din, x, ctx):
    m = Memory(nc, ctx, "x_")
    x["w1"] = [m.sb(f"w1{i}", [P, E, KD, 2 * F], F16) for i in range(2)]
    x["w2"] = [m.sb(f"w2{i}", [P, E, FC, D], F16) for i in range(2)]
    x["b1"] = m.sb("b1", [P, E, 2 * FC])
    x["b2"] = m.sb("b2", [P, E, D])
    with ExitStack() as inner:
        m = Memory(nc, inner, "xload_")
        stage = m.sb("stage", [P, 2, 2048])
        loaded, split, split_hi = m.counter("loaded"), m.counter("split"), m.counter("split_hi")
        bias_in, bias_up = m.counter("bias_in"), m.counter("bias_up")
        jobs = [(e, layer, n) for e in range(E) for layer, n in (("w1", KD * 2 * F), ("w2", FC * D))]
        src = {"w1": din["x_w1"], "w2": din["x_w2"]}
        block = inner.enter_context(nc.Block())

        @block.sync
        def _(sp):
            sp.dma_start(x["b1"][:], din["x_b1"]).then_inc(bias_in.sem, 16)
            sp.dma_start(x["b2"][:], din["x_b2"].rearrange("(a e) d -> a e d", a=1).to_broadcast([P, E, D])
                         ).then_inc(bias_in.sem, 16)
            for j, (e, layer, n) in enumerate(jobs):
                if j >= 2:
                    sp.wait_ge(split.sem, j - 1)
                sp.dma_start(stage[:, j % 2, 0:n].rearrange("p (k n) -> p k n", k=n // src[layer].shape[2]),
                             src[layer][e].rearrange("(k p) n -> p k n", p=P)).then_inc(loaded.sem, 16)
                sp.wait_ge(loaded.sem, 16 * (j + 1))
            sp.wait_ge(bias_in.sem, 32)

        @block.scalar
        def _(act):
            for j, (e, layer, n) in enumerate(jobs):
                act.wait_ge(loaded.sem, 16 * (j + 1))
                act.copy(x[layer][0][:, e, :, :].rearrange("p k n -> p (k n)"), stage[:, j % 2, 0:n]
                         ).then_inc(split_hi.sem, 1)

        @block.vector
        def _(dve):
            dve.wait_ge(bias_in.sem, 32)
            dve.tensor_scalar(x["b1"][:, :, FC:], x["b1"][:, :, FC:], 1.0, None, ALU.add).then_inc(bias_up.sem, 1)
            for j, (e, layer, n) in enumerate(jobs):
                dve.wait_ge(split_hi.sem, j + 1)
                dve.tensor_tensor(x[layer][1][:, e, :, :].rearrange("p k n -> p (k n)"), stage[:, j % 2, 0:n],
                                  x[layer][0][:, e, :, :].rearrange("p k n -> p (k n)"), ALU.subtract
                                  ).then_inc(split.sem, 1)


def experts(nc, w, x, keep, scratch, capacity, n_tiles):
    RT = ROWS // P
    last_row = (E * capacity) - ROWS
    with ExitStack() as ctx:
        m = Memory(nc, ctx, "experts_")
        rows = m.sb("rows", [P, 2, RT, 2 * D], F16)
        xT = m.sb("xT", [P, 2, 2, KD, ROWS], F16)
        g = m.sb("g", [P, 2, 2 * ROWS])
        sg = m.sb("sg", [P, 2, 2 * ROWS])
        v = m.sb("v", [P, 2, 2 * ROWS])
        hf = m.sb("hf", [P, 2, 2 * ROWS])
        h = [m.sb(n, [P, 2, FC, ROWS], F16) for n in ("hh", "hl")]
        y = m.sb("y", [P, 2, RT, D])
        pt = m.ps("pt", [P, 2 * KD, ROWS], F16)
        pg = m.ps("pg", [P, 2, 512])
        pv = m.ps("pv", [P, 2, 512])
        py = m.ps("py", [P, 2, 512])
        row_in = [m.counter(f"row_in{u}", 16) for u in range(2)]
        turned = m.counter("turned", 1)
        xT_sb = m.counter("xT_sb", 1)
        up_mm = m.counter("up_mm", 2)
        g_sb, v_sb = m.counter("g_sb", 4), m.counter("v_sb", 4)
        sig_sb, gs = m.counter("sig_sb", 2), m.counter("gs", 2)
        h_f, h_hi, h_lo = m.counter("h_f", 2), m.counter("h_hi", 2), m.counter("h_lo", 2)
        down_mm = m.counter("down_mm", 1)
        y_sb = m.counter("y_sb", 1)
        y_out = [m.counter(f"y_out{u}", 16) for u in range(2)]
        block = ctx.enter_context(nc.Block())

        def loop(eng, body):
            for i in range(2):
                for u in range(2):
                    body(i, u, i + u == 0, False)
            with eng.Fori(2, n_tiles // 2 - 1) as i:
                for u in range(2):
                    body(i, u, False, False)
            for u in range(2):
                body(n_tiles // 2 - 1, u, False, True)

        def expert_of(eng, tile):
            return eng.value_load(keep["tiles"][0:1, 0, bass.ds(tile, 1)], min_val=0, max_val=E - 1)

        def row_of(eng, tile):
            return eng.value_load(keep["tiles"][0:1, 1, bass.ds(tile, 1)], min_val=0, max_val=last_row)

        def flat(ap, u, q):
            return ap[:, u, 2 * q:2 * q + 2, :].rearrange("p f r -> p (f r)")

        @block.sync
        def _(sp):
            def load(tile, u):
                r = row_of(sp, tile)
                sp.dma_start(rows[:, u, :, :], scratch["queue"][bass.ds(r, ROWS), :].rearrange(
                    "(t p) d -> p t d", p=P)).then_inc(row_in[u].sem, 16)

            def store(tile, u):
                sp.wait_ge(y_sb.sem, y_sb.at(tile, 1))
                sp.dma_start(scratch["y"][bass.ds(tile * ROWS, ROWS), :].rearrange("(t p) d -> p t d", p=P),
                             y[:, u, :, :]).then_inc(y_out[u].sem, 16)

            def body(pair, u, first, ending):
                tile = pair * 2 + u
                if not ending:
                    sp.wait_ge(turned.sem, turned.at(tile, 1))
                    load(tile + 2, u)
                if not first:
                    store(tile - 1, 1 - u)

            load(0, 0)
            load(1, 1)
            loop(sp, body)
            store(n_tiles - 1, 1)
            for u in range(2):
                sp.wait_ge(y_out[u].sem, y_out[u].at(n_tiles // 2, 0))

        @block.tensor
        def _(pe):
            def turn(pair, u):
                tile = pair * 2 + u
                pe.wait_ge(row_in[u].sem, row_in[u].at(pair, 16))
                pe.wait_ge(xT_sb.sem, xT_sb.at(tile, 0))
                for t in range(RT):
                    for i in range(2):
                        for k in range(KD):
                            last = pe.transpose(pt[:, i * KD + k, t * P:(t + 1) * P],
                                                rows[:, u, t, (i * KD + k) * P:(i * KD + k + 1) * P],
                                                w["identh"][:])
                last.then_inc(turned.sem, 1)

            def up(tile, u):
                e = expert_of(pe, tile)
                pe.wait_ge(xT_sb.sem, xT_sb.at(tile, 1))
                for q in range(2):
                    pe.wait_ge(g_sb.sem, g_sb.at(tile - 1, 2 * q + 2))
                    pe.wait_ge(v_sb.sem, v_sb.at(tile - 1, 2 * q + 2))
                    for part, bank in ((0, pg), (1, pv)):
                        for f in range(2):
                            col = part * F + (2 * q + f) * P
                            for k in range(KD):
                                last = hi_lo_products(
                                    pe, bank[:, q, f * ROWS:(f + 1) * ROWS],
                                    [a[:, bass.ds(e, 1), k, col:col + P].rearrange("p a n -> p (a n)")
                                     for a in x["w1"]],
                                    [xT[:, u, i, k, :] for i in range(2)], k == 0, k == KD - 1)
                    last.then_inc(up_mm.sem, 1)

            def down(tile, u):
                e = expert_of(pe, tile)
                pe.wait_ge(h_lo.sem, h_lo.at(tile, 2))
                pe.wait_ge(y_sb.sem, y_sb.at(tile - 1, 0))
                for t in range(RT):
                    for f in range(FC):
                        last = hi_lo_products(
                            pe, py[:, u, t * D:(t + 1) * D], [a[:, u, f, t * P:(t + 1) * P] for a in h],
                            [a[:, bass.ds(e, 1), f, :].rearrange("p a n -> p (a n)") for a in x["w2"]],
                            f == 0, f == FC - 1)
                last.then_inc(down_mm.sem, 1)

            def body(pair, u, first, ending):
                tile = pair * 2 + u
                up(tile, u)
                if not ending:
                    turn(pair + 1, u)
                if not first:
                    down(tile - 1, 1 - u)

            turn(0, 0)
            turn(0, 1)
            loop(pe, body)
            down(n_tiles - 1, 1)

        @block.scalar
        def _(act):
            def copy_rows(tile, u):
                act.wait_ge(turned.sem, turned.at(tile, 1))
                act.copy(xT[:, u, :, :, :].rearrange("p i k r -> p (i k) r"), pt[:]).then_inc(xT_sb.sem, 1)

            def body(pair, u, first, ending):
                tile = pair * 2 + u

                def sigmoid(q):
                    act.wait_ge(h_f.sem, h_f.at(tile - 1, q + 1))
                    act.wait_ge(g_sb.sem, g_sb.at(tile, 2 * q + 2))
                    act.activation(sg[:, q, :], g[:, q, :], ACT.Sigmoid, scale=1.702).then_inc(sig_sb.sem, 1)

                def high(q):
                    act.wait_ge(down_mm.sem, down_mm.at(tile - 1, 0))
                    act.wait_ge(h_f.sem, h_f.at(tile, q + 1))
                    act.copy(flat(h[0], u, q), hf[:, q, :]).then_inc(h_hi.sem, 1)

                sigmoid(0)
                high(0)
                sigmoid(1)
                if not ending:
                    copy_rows(tile + 2, u)
                high(1)

            copy_rows(0, 0)
            copy_rows(1, 1)
            loop(act, body)

        @block.vector
        def _(dve):
            def body(pair, u, first, ending):
                tile = pair * 2 + u
                e = expert_of(dve, tile)

                def gates_and_values(q):
                    dve.wait_ge(gs.sem, gs.at(tile - 1, q + 1))
                    dve.wait_ge(h_f.sem, h_f.at(tile - 1, q + 1))
                    dve.wait_ge(up_mm.sem, up_mm.at(tile, q + 1))
                    for dst, bank, bias, top, done in ((g, pg, 0, 9.0, g_sb), (v, pv, FC, 10.0, v_sb)):
                        for f in range(2):
                            dve.tensor_scalar(dst[:, q, f * ROWS:(f + 1) * ROWS], bank[:, q, f * ROWS:(f + 1) * ROWS],
                                              x["b1"][:, bass.ds(e, 1), bias + 2 * q + f], top, ALU.add, ALU.min
                                              ).then_inc(done.sem, 1)

                def hidden(q):
                    dve.wait_ge(gs.sem, gs.at(tile, q + 1))
                    dve.wait_ge(v_sb.sem, v_sb.at(tile, 2 * q + 2))
                    dve.wait_ge(h_lo.sem, h_lo.at(tile - 1, q + 1))
                    dve.scalar_tensor_tensor(out=hf[:, q, :], in0=v[:, q, :], scalar=-8.0, in1=sg[:, q, :],
                                             op0=ALU.max, op1=ALU.mult).then_inc(h_f.sem, 1)

                def low(q):
                    dve.wait_ge(h_hi.sem, h_hi.at(tile, q + 1))
                    dve.tensor_tensor(flat(h[1], u, q), hf[:, q, :], flat(h[0], u, q), ALU.subtract
                                      ).then_inc(h_lo.sem, 1)

                gates_and_values(0)
                hidden(0)
                gates_and_values(1)
                low(0)
                hidden(1)
                if not first:
                    add_bias(pair - 1 + u, tile - 1, 1 - u)
                low(1)

            def add_bias(pair, tile, u):
                e = expert_of(dve, tile)
                dve.wait_ge(down_mm.sem, down_mm.at(tile, 1))
                dve.wait_ge(y_out[u].sem, y_out[u].at(pair, 0))
                dve.tensor_tensor(y[:, u, :, :], py[:, u, :].rearrange("p (t d) -> p t d", t=RT),
                                  x["b2"][:, bass.ds(e, 1), :].to_broadcast([P, RT, D]), ALU.add
                                  ).then_inc(y_sb.sem, 1)

            loop(dve, body)
            add_bias(n_tiles // 2 - 1, n_tiles - 1, 1)

        @block.gpsimd
        def _(pool):
            def body(pair, u, first, ending):
                tile = pair * 2 + u
                for q in range(2):
                    pool.wait_ge(sig_sb.sem, sig_sb.at(tile, q + 1))
                    pool.tensor_tensor(sg[:, q, :], sg[:, q, :], g[:, q, :], ALU.mult).then_inc(gs.sem, 1)

            loop(pool, body)



def combine(nc, din, keep, scratch, out, NB):
    with ExitStack() as ctx:
        m = Memory(nc, ctx, "combine_")
        n_pairs = NB * TT
        p = m.sb("p", [P, n_pairs, 2])
        total = m.sb("total", [P, n_pairs])
        slot = m.sb("slot", [P, 2, 2 * TT], I32)
        pb = m.sb("pb", [P, 2, 2 * TT])
        y = m.sb("y", [P, 2, 2 * TT, D])
        x2 = m.sb("x2", [P, 2, TT, D])
        gb = m.sb("gb", [P, 2, 1, D])
        acc = m.sb("acc", [P, 2, TT, D])
        shifted, exped, weighed = m.counter("shifted"), m.counter("exped"), m.counter("weighed")
        passed = m.counter("passed")
        by_parity = lambda name, per: [m.counter(f"{name}{u}", per) for u in range(2)]
        x2_in = by_parity("x2_in", 32)
        slot_sb = by_parity("slot_sb", 1)
        y_in = by_parity("y_in", 16 * 2 * TT)
        p_sb = by_parity("p_sb", 1)
        first, both = by_parity("first", TT), by_parity("both", TT)
        gated, summed = by_parity("gated", 1), by_parity("summed", 1)
        out_done = by_parity("out_done", 16)
        block = ctx.enter_context(nc.Block())

        def loop(eng, body):
            for u in range(2):
                body(0, u, u)
            if NB > 4:
                with eng.Fori(1, NB // 2 - 1) as pair:
                    for u in range(2):
                        body(pair, u, pair * 2 + u)
            for u in range(2):
                body(NB // 2 - 1, u, NB - 2 + u)

        def rows_of(ap, b):
            return ap[bass.ds(b, 1), :, :].rearrange("a (t p) d -> p (a t) d", p=P)

        @block.sync
        def _(sp):
            def load(pair, u, b):
                sp.wait_ge(summed[u].sem, summed[u].at(pair, 0))
                sp.dma_start(x2[:, u, :, :], rows_of(scratch["x2"], b)).then_inc(x2_in[u].sem, 16)
                sp.dma_start(gb[:, u, :, :], scratch["mod"][bass.ds(b, 1), 5 * D:6 * D].rearrange(
                    "a (i d) -> a i d", i=1).to_broadcast([P, 1, D])).then_inc(x2_in[u].sem, 16)

            loop(sp, load)

        @block.scalar
        def _(act):
            act.wait_ge(shifted.sem, 1)
            act.activation(p[:], p[:], ACT.Exp).then_inc(exped.sem, 1)

            def store(pair, u, b):
                act.wait_ge(summed[u].sem, summed[u].at(pair, 1))
                act.dma_start(rows_of(out, b), acc[:, u, :, :]).then_inc(out_done[u].sem, 16)

            loop(act, store)
            for u in range(2):
                act.wait_ge(out_done[u].sem, out_done[u].at(NB // 2, 0))

        @block.gpsimd
        def _(pool):
            def gather(pair, u, b):
                pool.wait_ge(both[u].sem, both[u].at(pair, 0))
                pool.tensor_copy(slot[:, u, :], keep["rows"][:, bass.ds(b * 2 * TT, 2 * TT)]
                                 ).then_inc(slot_sb[u].sem, 1)
                wait_alone(pool, slot_sb[u].sem, slot_sb[u].at(pair, 1), passed)
                for j in range(2 * TT):
                    pool.indirect_dma_start(out=y[:, u, j, :], out_offset=None, in_=scratch["y"],
                                            in_offset=bass.IndirectOffsetOnAxis(ap=slot[:, u, j:j + 1], axis=0)
                                            ).then_inc(y_in[u].sem, 16)

            loop(pool, gather)

        @block.vector
        def _(dve):
            lead = keep["top"][:, :, 0:1].to_broadcast([P, n_pairs, 2])
            dve.tensor_tensor(p[:], keep["top"][:], lead, ALU.subtract).then_inc(shifted.sem, 1)
            dve.wait_ge(exped.sem, 1)
            dve.tensor_reduce(total[:], p[:], AX.X, ALU.add).then_inc(weighed.sem, 1)
            dve.wait_ge(weighed.sem, 1)
            dve.reciprocal(total[:], total[:]).then_inc(weighed.sem, 1)
            dve.wait_ge(weighed.sem, 2)
            dve.tensor_tensor(p[:], p[:], total[:].unsqueeze(2).to_broadcast([P, n_pairs, 2]), ALU.mult
                              ).then_inc(weighed.sem, 1)
            dve.wait_ge(weighed.sem, 3)

            def blend(pair, u, b):
                dve.wait_ge(both[u].sem, both[u].at(pair, 0))
                dve.tensor_copy(pb[:, u, :].rearrange("p (t k) -> p t k", k=2), p[:, bass.ds(b * TT, TT), :]
                                ).then_inc(p_sb[u].sem, 1)
                dve.wait_ge(p_sb[u].sem, p_sb[u].at(pair, 1))
                dve.wait_ge(y_in[u].sem, y_in[u].at(pair + 1, 0))
                dve.wait_ge(out_done[u].sem, out_done[u].at(pair, 0))
                for t in range(TT):
                    dve.tensor_scalar(acc[:, u, t, :], y[:, u, 2 * t, :], pb[:, u, 2 * t:2 * t + 1], None, ALU.mult
                                      ).then_inc(first[u].sem, 1)
                for t in range(TT):
                    dve.wait_ge(first[u].sem, first[u].at(pair, t + 1))
                    dve.scalar_tensor_tensor(out=acc[:, u, t, :], in0=y[:, u, 2 * t + 1, :],
                                             scalar=pb[:, u, 2 * t + 1:2 * t + 2], in1=acc[:, u, t, :],
                                             op0=ALU.mult, op1=ALU.add).then_inc(both[u].sem, 1)
                dve.wait_ge(both[u].sem, both[u].at(pair + 1, 0))
                dve.wait_ge(x2_in[u].sem, x2_in[u].at(pair + 1, 0))
                dve.tensor_tensor(acc[:, u, :, :], acc[:, u, :, :], gb[:, u, :, :].to_broadcast([P, TT, D]), ALU.mult
                                  ).then_inc(gated[u].sem, 1)
                dve.wait_ge(gated[u].sem, gated[u].at(pair, 1))
                dve.tensor_tensor(acc[:, u, :, :], acc[:, u, :, :], x2[:, u, :, :], ALU.add
                                  ).then_inc(summed[u].sem, 1)

            loop(dve, blend)


def n_tiles(NB):
    n = 2 * NB * L // ROWS + E - 1
    return n + n % 2


def program(nc, din, out, scratch, NB):
    capacity = NB * L + ROWS
    with ExitStack() as ctx:
        m = Memory(nc, ctx, "w_")
        w = {}
        keep = {"base": m.sb("base", [P, E]), "top": m.sb("top", [P, NB * TT, 2]),
                "slots": m.sb("slots", [P, NB * 2 * TT]), "rows": m.sb("rows", [P, NB * 2 * TT], I32), "tiles": m.sb("tiles", [1, 2, n_tiles(NB)], I32)}

        def const(name, shape, dt=F32):
            w[name] = m.sb(name, shape, dt)

        def halves(name, k, n):
            w[name] = [m.sb(f"{name}_{part}", [P, k, n], F16) for part in ("hi", "lo")]

        const("identf", [P, P])
        const("identb", [P, P], BF16)
        const("identh", [P, P], F16)
        with ExitStack() as dense:
            m = Memory(nc, dense, "w_")
            halves("gate", KD, E)
            const("ones3", [3, P], BF16)
            const("ones", [P, P], BF16)
            const("before", [P, P], BF16)
            const("b23", [3, D], BF16)
            for name, k in (("g1", KD), ("b1", KD), ("g2", KD), ("b2", KD), ("mb1", FMC), ("bu", 1), ("A", 1)):
                const(name, [P, k])
            halves("w1", KD, FM)
            halves("w2", FMC, D)
            with ExitStack() as mixer_only:
                m = Memory(nc, mixer_only, "w_")
                halves("qk", KD, 2 * D)
                halves("v", KD, D)
                halves("g", KD, D)
                halves("drive", KD, S)
                halves("o", 2, D)
                halves("c", 1, D)
                halves("nc", 1, D)
                for name in ("bg3", "bo3"):
                    const(name, [3, D], BF16)
                const("twoI", [P, P], BF16)
                const("parity", [P, 2])
                const("maskq", [P, 2, 4, P], BF16)
                const("select", [P, 2, PAIRS, P], BF16)
                const("shift", [P, 2, P], BF16)
                const("mx", [P, 2, P], BF16)
                for name in ("xTh", "xTl"):
                    const(name, [P, KD, WIN + L], F16)
                const("Kz", [P, 4, 2, 2, WIN + L], F16)
                const("V", [P, NW, PAIRS, 2 * DH + 1])
                setup(nc, din, w, scratch)
                mixer(nc, din, w, scratch, NB)
            mlp(nc, din, w, scratch, NB, keep, capacity)
        x = {}
        plan(nc, keep, scratch, capacity, n_tiles(NB))
        with ExitStack() as weights:
            expert_weights(nc, din, x, weights)
            experts(nc, w, x, keep, scratch, capacity, n_tiles(NB))
        combine(nc, din, keep, scratch, out, NB)


def launch_arrays(inputs):
    import numpy as np

    a = {name.removeprefix("L0_").removeprefix("attn_"): np.asarray(v) for name, v in inputs.items()}
    column = lambda v, k: v.reshape(k, P).T
    NB = a["x"].shape[0]
    w1 = a["ffn_dense_1_w"].transpose(0, 2, 1)
    b1 = a["ffn_dense_1_b"]
    arrays = {
        "x": a["x"], "cT": a["c"].T.reshape(KD, P, NB).transpose(1, 0, 2), "wmod": a["wmod"],
        "Wqk": a["W_qkv"][:, :2 * D], "Wv": a["W_qkv"][:, 2 * D:], "Wu": a["W_ug"][:, :S], "Wg": a["W_ug"][:, S:],
        "b_u": column(a["b_ug"][:S], 1), "b_g": a["b_ug"][S:], "Bw": a["B_w"], "A": column(a["A"], 1),
        "Cw": a["C_w"], "b_O": a["b_O"],
        "WO": a["W_O"].reshape(PAIRS, 2, DH, D).transpose(1, 0, 2, 3).reshape(D, D),
        "ln1_g": column(a["ln1_g"], KD), "ln1_b": column(a["ln1_b"], KD),
        "ln2_g": column(a["ln2_g"], KD), "ln2_b": column(a["ln2_b"], KD),
        "W1": a["mlp_W1"], "mlp_b1": column(a["mlp_b1"], FMC), "W2": a["mlp_W2"], "mlp_b2": a["mlp_b2"],
        "gate_w": a["ffn_gate_w"],
        "x_w1": np.concatenate([w1[:, :, 0::2], w1[:, :, 1::2]], 2),
        "x_b1": np.concatenate([b1[:, 0::2], b1[:, 1::2]], 1).reshape(E, 2 * FC, P).transpose(2, 0, 1),
        "x_w2": a["ffn_dense_2_w"].transpose(0, 2, 1), "x_b2": a["ffn_dense_2_b"],
    }
    return {name: np.ascontiguousarray(v) for name, v in arrays.items()}


def build(nc, arrays):
    NB = arrays["x"].shape[0]
    capacity = NB * L + ROWS
    din = {n: nc.dram_tensor(f"in_{n}", v.shape, mybir.dt.from_np(v.dtype), kind="ExternalInput").ap()
           for n, v in arrays.items()}
    out = nc.dram_tensor("out", (NB, L, D), F32, kind="ExternalOutput").ap()
    scratch = {}
    for name, shape, dt in (("mod", (NB, 6 * D), F32), ("x1", (NB, L, D), F32), ("x2", (NB, L, D), F32),
                            ("queue", (E * capacity, 2 * D), F16), ("y", (n_tiles(NB) * ROWS, D), F32)):
        scratch[name] = nc.dram_tensor(f"scratch_{name}", shape, dt).ap()
    program(nc, din, out, scratch, NB)


def kernel(**inputs):
    import concourse.bacc as _bacc
    from concourse.bass_utils import run_bass_kernel_spmd as _run

    nc = _bacc.Bacc("TRN2", target_bir_lowering=False, num_devices=1)
    arrays = launch_arrays(inputs)
    build(nc, arrays)
    r = _run(nc, [{f"in_{n}": v for n, v in arrays.items()}], core_ids=[0])
    return r.results[0]["out"]
```

```python
from contextlib import ExitStack

import concourse.bass as bass
from concourse import mybir

ALU = mybir.AluOpType
ACT = mybir.ActivationFunctionType
AX = mybir.AxisListType
F32 = mybir.dt.float32
F16 = mybir.dt.float16
BF16 = mybir.dt.bfloat16
I32 = mybir.dt.int32
U32 = mybir.dt.uint32

P = 128
D = 256
KD = D // P
L = 512
TT = L // P
WIN = 64
NW = L // WIN
H = 16
DH = D // H
PAIRS = H // 2
S = 128
FM = 4 * D
FMC = FM // P
E = 8
F = 512
FC = F // P
EPS = 1e-5
MASKED = -1e30
SCALE = DH ** -0.5
SEED, NEWTON = 3, 12
ROOT = 13
PIECE = 2 * F + FC // 2 * D
ROWS = 256


class Counter:

    def __init__(self, sem, per):
        self.sem, self.per = sem, per

    def at(self, i, n):
        return max(i * self.per + n, 0) if isinstance(i, int) else i * self.per + n


class Memory:

    def __init__(self, nc, ctx, phase):
        self.nc, self.ctx, self.phase = nc, ctx, phase

    def sb(self, name, shape, dt=F32):
        return self.ctx.enter_context(self.nc.sbuf_tensor(self.phase + name, shape, dt))

    def ps(self, name, shape, dt=F32):
        return self.ctx.enter_context(self.nc.psum_tensor(self.phase + name, shape, dt))

    def counter(self, name, per=1):
        return Counter(self.ctx.enter_context(self.nc.semaphore(self.phase + name)), per)


def wait_alone(eng, sem, value, passed):
    eng.wait_ge(sem, value).then_inc(passed.sem, 1)


def seed_inverse_root(dve, sig, i, n, var, v, y):
    dve.tensor_scalar(v, var, EPS, None, ALU.add).then_inc(sig.sem, 1)
    dve.wait_ge(sig.sem, sig.at(i, n + 1))
    dve.tensor_scalar(y.bitcast(I32), v.bitcast(I32), 1, None, ALU.logical_shift_right).then_inc(sig.sem, 1)
    dve.wait_ge(sig.sem, sig.at(i, n + 2))
    dve.tensor_scalar(y.bitcast(I32), y.bitcast(I32), -1.0, float(0x5F3759DF), ALU.mult, ALU.add
                      ).then_inc(sig.sem, 1)


def refine_inverse_root(pool, sig, i, n, v, y, a, passed):
    for _ in range(3):
        for op in (lambda: pool.tensor_tensor(a, y, y, ALU.mult),
                   lambda: pool.tensor_tensor(a, a, v, ALU.mult),
                   lambda: pool.tensor_scalar(a, a, -0.5, 1.5, ALU.mult, ALU.add),
                   lambda: pool.tensor_tensor(y, y, a, ALU.mult)):
            op().then_inc(sig.sem, 1)
            n += 1
            wait_alone(pool, sig.sem, sig.at(i, n), passed)


def inverse_root(dve, sig, i, var, v, y, a):
    n = 0
    steps = [lambda: dve.tensor_scalar(v, var, EPS, None, ALU.add),
             lambda: dve.tensor_scalar(y.bitcast(I32), v.bitcast(I32), 1, None, ALU.logical_shift_right),
             lambda: dve.tensor_scalar(y.bitcast(I32), y.bitcast(I32), -1.0, float(0x5F3759DF), ALU.mult, ALU.add),
             lambda: dve.tensor_scalar(v, v, -0.5, None, ALU.mult)]
    for _ in range(3):
        steps += [lambda: dve.tensor_tensor(a, y, y, ALU.mult),
                  lambda: dve.tensor_tensor(a, a, v, ALU.mult),
                  lambda: dve.scalar_tensor_tensor(out=y, in0=a, scalar=1.5, in1=y, op0=ALU.add, op1=ALU.mult)]
    for step in steps:
        step().then_inc(sig.sem, 1)
        n += 1
        dve.wait_ge(sig.sem, sig.at(i, n))


def hi_lo_products(pe, out, lhs, rhs, start, stop):
    pe.matmul(out, lhs[0], rhs[0], start=start, stop=False)
    pe.matmul(out, lhs[0], rhs[1], start=False, stop=False)
    return pe.matmul(out, lhs[1], rhs[0], start=False, stop=stop)



def setup(nc, din, w, scratch):
    NB = din["cT"].shape[2]
    jobs = [
        (w["qk"], din["Wqk"], None), (w["v"], din["Wv"], None), (w["g"], din["Wg"], None),
        (w["drive"], din["Bw"], din["Wu"]), (w["o"], din["WO"], None), (w["c"], din["Cw"], None),
        (w["w1"], din["W1"], None), (w["w2"], din["W2"], None), (w["gate"], din["gate_w"], None),
    ]
    rows = [(w["bg3"], din["b_g"]), (w["bo3"], din["b_O"]), (w["b23"], din["mlp_b2"])]
    with ExitStack() as ctx:
        m = Memory(nc, ctx, "setup_")
        stage = m.sb("stage", [P, 2, 2048])
        added = m.sb("added", [P, 256])
        wmod = m.sb("wmod", [P, KD, 6 * D])
        cT = m.sb("cT", [P, KD, NB])
        th = m.sb("th", [P, KD, NB])
        sc = m.sb("sc", [P, KD, NB])
        mod = m.sb("mod", [NB, 6 * D])
        sgn = m.sb("sgn", [NB, D])
        neg = m.sb("neg", [NB, D])
        maskg = m.sb("maskg", [P, 2, 4])
        brow = m.sb("brow", [1, 3, D])
        parts = m.sb("parts", [1, 3, 3, D], BF16)
        pm = [m.ps(f"pm{i}", [P, 512]) for i in range(3)]
        loaded = m.counter("loaded")
        vloaded = m.counter("vloaded")
        cloaded = m.counter("cloaded")
        bloaded = m.counter("bloaded")
        splitting = m.counter("splitting")
        split = m.counter("split")
        summed = m.counter("summed")
        tanh_c = m.counter("tanh_c")
        silu_c = m.counter("silu_c")
        mod_mm = m.counter("mod_mm")
        mod_sb = m.counter("mod_sb")
        mod_out = m.counter("mod_out")
        bsplit = m.counter("bsplit")
        filled = m.counter("filled")
        grouped = m.counter("grouped")
        shaped = m.counter("shaped")
        copied = m.counter("copied")
        bparts = m.counter("bparts")
        block = ctx.enter_context(nc.Block())

        @block.sync
        def _(sp):
            sp.dma_start(cT[:], din["cT"]).then_inc(cloaded.sem, 16)
            sp.dma_start(wmod[:], din["wmod"].rearrange("(k p) n -> p k n", p=P)).then_inc(cloaded.sem, 16)
            for j, (_, b) in enumerate(rows):
                sp.dma_start(brow[:, j, :], b.rearrange("(a n) -> a n", a=1)).then_inc(bloaded.sem, 16)
            for j, (dst, src, k) in enumerate([
                    (w["g1"], din["ln1_g"], KD), (w["b1"], din["ln1_b"], KD), (w["g2"], din["ln2_g"], KD),
                    (w["b2"], din["ln2_b"], KD), (w["mb1"], din["mlp_b1"], FMC), (w["bu"], din["b_u"], 1),
                    (w["A"], din["A"], 1)]):
                sp.dma_start(dst[:], src).then_inc(vloaded.sem, 16)
            for j, (dst, src, plus) in enumerate(jobs):
                n = dst[0].shape[1] * dst[0].shape[2]
                if j >= 2:
                    sp.wait_ge(split.sem, j - 1)
                view = stage[:, j % 2, 0:n].rearrange("p (k n) -> p k n", k=dst[0].shape[1])
                sp.dma_start(view, src.rearrange("(k p) n -> p k n", p=P)).then_inc(loaded.sem, 16)
                if plus is not None:
                    sp.dma_start(added[:, 0:n].rearrange("p (k n) -> p k n", k=dst[0].shape[1]),
                                 plus.rearrange("(k p) n -> p k n", p=P)).then_inc(loaded.sem, 16)
                sp.wait_ge(loaded.sem, 16 * (j + 1) + (16 if j >= 3 else 0))
            sp.wait_ge(vloaded.sem, 16 * 7)
            sp.wait_ge(bparts.sem, 3)
            for j, (dst, _) in enumerate(rows):
                for q in range(3):
                    sp.dma_start(dst[q:q + 1, :], parts[:, j, q, :]).then_inc(bsplit.sem, 16)
            sp.wait_ge(bsplit.sem, 16 * 9)
            sp.wait_ge(mod_sb.sem, 13)
            sp.dma_start(scratch["mod"], mod[:]).then_inc(mod_out.sem, 16)
            sp.wait_ge(mod_out.sem, 16)

        @block.scalar
        def _(act):
            act.wait_ge(cloaded.sem, 32)
            act.activation(th[:], cT[:], ACT.Tanh, scale=0.5).then_inc(tanh_c.sem, 1)

        @block.tensor
        def _(pe):
            pe.wait_ge(silu_c.sem, 2)
            for n in range(3):
                for k in range(KD):
                    last = pe.matmul(pm[n][0:NB, :], sc[:, k, :], wmod[:, k, n * 512:(n + 1) * 512],
                                     start=(k == 0), stop=(k == KD - 1))
                last.then_inc(mod_mm.sem, 1)

        @block.vector
        def _(dve):
            dve.wait_ge(tanh_c.sem, 1)
            dve.scalar_tensor_tensor(out=sc[:], in0=th[:], scalar=1.0, in1=cT[:], op0=ALU.add,
                                     op1=ALU.mult).then_inc(silu_c.sem, 1)
            dve.wait_ge(silu_c.sem, 1)
            dve.tensor_scalar(sc[:], sc[:], 0.5, None, ALU.mult).then_inc(silu_c.sem, 1)
            for n in range(3):
                dve.wait_ge(mod_mm.sem, n + 1)
                dve.tensor_copy(mod[:, n * 512:(n + 1) * 512], pm[n][0:NB, :]).then_inc(mod_sb.sem, 1)
            for half in range(2):
                dve.wait_ge(mod_sb.sem, 3 + 5 * half)
                scale_, gate_ = (mod[:, (3 * half + i) * D:(3 * half + i + 1) * D] for i in (1, 2))
                dve.tensor_scalar(scale_, scale_, 1.0, None, ALU.add).then_inc(mod_sb.sem, 1)
                dve.tensor_scalar(sgn[:], gate_, 0.0, 2.0, ALU.is_ge, ALU.mult).then_inc(mod_sb.sem, 1)
                dve.tensor_scalar(neg[:], gate_, -1.0, None, ALU.mult).then_inc(mod_sb.sem, 1)
                dve.wait_ge(mod_sb.sem, 6 + 5 * half)
                dve.scalar_tensor_tensor(out=gate_, in0=neg[:], scalar=0.25, in1=gate_, op0=ALU.max,
                                         op1=ALU.max).then_inc(mod_sb.sem, 1)
                dve.wait_ge(mod_sb.sem, 7 + 5 * half)
                dve.scalar_tensor_tensor(out=gate_, in0=sgn[:], scalar=-1.0, in1=gate_, op0=ALU.add,
                                         op1=ALU.mult).then_inc(mod_sb.sem, 1)
            dve.wait_ge(bloaded.sem, 48)
            for q in range(3):
                dve.tensor_copy(parts[:, :, q, :], brow[:]).then_inc(bparts.sem, 1)
                dve.wait_ge(bparts.sem, q + 1)
                if q < 2:
                    dve.tensor_tensor(brow[:], brow[:], parts[:, :, q, :], ALU.subtract).then_inc(shaped.sem, 1)
                    dve.wait_ge(shaped.sem, q + 1)
            for j, (dst, _, plus) in enumerate(jobs):
                hi, lo = dst[0], dst[1]
                k = hi.shape[1]
                n = k * hi.shape[2]
                src = stage[:, j % 2, 0:n].rearrange("p (k n) -> p k n", k=k)
                dve.wait_ge(loaded.sem, 16 * (j + 1) + (16 if j >= 3 else 0))
                if plus is not None:
                    dve.tensor_tensor(src, src, added[:, 0:n].rearrange("p (k n) -> p k n", k=k),
                                      ALU.add).then_inc(summed.sem, 1)
                    dve.wait_ge(summed.sem, 1)
                dve.tensor_copy(hi[:], src).then_inc(splitting.sem, 1)
                dve.wait_ge(splitting.sem, j + 1)
                dve.tensor_tensor(lo[:], src, hi[:], ALU.subtract).then_inc(split.sem, 1)
            dve.wait_ge(grouped.sem, 1)
            dve.tensor_reduce(w["parity"][:], maskg[:], AX.X, ALU.add).then_inc(shaped.sem, 1)
            dve.wait_ge(split.sem, len(jobs))
            for part in range(2):
                dve.tensor_scalar(w["nc"][part][:], w["c"][part][:], -1.0, None, ALU.mult).then_inc(shaped.sem, 1)

        @block.gpsimd
        def _(pool):
            n = 0

            def step(ins):
                nonlocal n
                n += 1
                ins.then_inc(filled.sem, 1)
                pool.wait_ge(filled.sem, n)

            step(pool.memset(w["identf"][:], 1.0))
            step(pool.affine_select(out=w["identf"][:], in_=w["identf"][:], compare_op=ALU.is_equal, fill=0.0,
                                    base=0, pattern=[[-1, P]], channel_multiplier=1))
            for name in ("identb", "identh"):
                step(pool.tensor_copy(w[name][:], w["identf"][:]))
            step(pool.memset(w["ones3"][:], 1.0))
            for name in ("twoI", "maskq", "select", "shift"):
                step(pool.memset(w[name][:], 0.0))
            step(pool.tensor_copy(w["twoI"][0:WIN, 0:WIN], w["identf"][0:WIN, 0:WIN]))
            step(pool.tensor_copy(w["twoI"][0:WIN, WIN:P], w["identf"][0:WIN, 0:WIN]))
            step(pool.memset(maskg[:], 1.0))
            for par in range(2):
                v = maskg[:, par, :]
                step(pool.affine_select(out=v, in_=v, compare_op=ALU.is_ge, fill=0.0, base=-DH * par,
                                        pattern=[[-2 * DH, 4]], channel_multiplier=1))
                step(pool.affine_select(out=v, in_=v, compare_op=ALU.is_ge, fill=0.0, base=DH * par + DH - 1,
                                        pattern=[[2 * DH, 4]], channel_multiplier=-1))
            pool.sem_inc(grouped.sem, 1)
            for var in range(2):
                v = w["maskq"][0:WIN, var, :, :]
                step(pool.affine_select(out=v, in_=v, compare_op=ALU.is_gt, fill=MASKED, base=0,
                                        pattern=[[0, 4], [1, P]], channel_multiplier=-1))
                step(pool.affine_select(out=v, in_=v, compare_op=ALU.is_ge, fill=MASKED, base=WIN,
                                        pattern=[[0, 4], [-1, P]], channel_multiplier=1))
                if var == 1:
                    step(pool.affine_select(out=v, in_=v, compare_op=ALU.is_ge, fill=MASKED, base=-WIN,
                                            pattern=[[0, 4], [1, P]], channel_multiplier=0))
                s = w["select"][0:WIN + PAIRS, var, :, :]
                step(pool.memset(s, -1.0))
                step(pool.affine_select(out=s, in_=s, compare_op=ALU.is_equal, fill=0.0, base=-WIN,
                                        pattern=[[-1, PAIRS], [0, P]], channel_multiplier=1))
                for i in range(PAIRS):
                    step(pool.tensor_copy(w["select"][0:WIN, var, i, :], w["maskq"][0:WIN, var, 0, :]))
            for b in range(2):
                step(pool.tensor_copy(w["shift"][0:WIN, b, :], w["twoI"][0:WIN, :]))
            step(pool.memset(w["before"][:], 1.0))
            step(pool.affine_select(out=w["before"][:], in_=w["before"][:], compare_op=ALU.is_gt, fill=0.0,
                                    base=0, pattern=[[1, P]], channel_multiplier=-1))
            step(pool.memset(w["ones"][:], 1.0))
            for name in ("xTh", "xTl"):
                step(pool.memset(w[name][:, :, 0:WIN], 0.0))
            step(pool.memset(w["Kz"][:].bitcast(F32), 0.0))
            step(pool.memset(w["mx"][:], 0.0))
            step(pool.memset(w["V"][:, :, :, 2 * DH:2 * DH + 1], 1.0))



def mixer(nc, din, w, scratch, NB):
    with ExitStack() as ctx:
        m = Memory(nc, ctx, "mixer_")
        x = m.sb("x", [P, TT, D])
        shsc = m.sb("shsc", [P, 2, D])
        nrm = m.sb("nrm", [P, TT, D])
        h = m.sb("h", [P, TT, D])
        hres = m.sb("hres", [P, TT, D])
        stats = m.sb("stats", [P, TT, 6])
        mv = m.sb("mv", [P, TT, 2])
        ve = m.sb("ve", [P, TT])
        rs = m.sb("rs", [P, TT])
        nt = m.sb("nt", [P, TT])
        xTf = m.sb("xTf", [P, KD, L])
        Qh = m.sb("Qh", [P, 2, NW, 2, WIN], F16)
        Ql = m.sb("Ql", [P, 2, NW, 2, WIN], F16)
        xTh, xTl, V, mx = (w[n] for n in ("xTh", "xTl", "V", "mx"))
        Kt = m.sb("Kt", [P, 2, 2, L], F16)
        Kz = w["Kz"]
        drv = m.sb("drv", [P, L])
        st = m.sb("st", [P, L])
        sth = m.sb("sth", [P, L], F16)
        stl = m.sb("stl", [P, L], F16)
        prob = m.sb("prob", [P, 2, PAIRS * P])
        rden = m.sb("rden", [P, 2, PAIRS])
        on = m.sb("on", [P, 2, PAIRS, DH])
        oTh = m.sb("oTh", [P, 2, L], F16)
        oTl = m.sb("oTl", [P, 2, L], F16)
        mix = m.sb("mix", [P, TT, D])
        x1 = m.sb("x1", [P, TT, D])
        sc = m.ps("sc", [P, 4, 512])
        pj = m.ps("pj", [P, 2, 512])
        pv = m.ps("pv", [P, 512])
        pm = m.ps("pm", [P, 512])
        maxT = pm[:, 0:P // 2].bitcast(BF16)
        q_bank = [pj[:, 0, :], pj[:, 1, :]]
        k_bank = [sc[:, 0, :], sc[:, 1, :]]
        drive_bank = sc[:, 2, :]
        v_bank = [sc[:, 3, :], pj[:, 0, :], pj[:, 1, :], sc[:, 2, :]]
        y_bank = [pm[:, 0:D], pv[:, 0:D]]

        x_in = m.counter("x_in", 32)
        dve_passed, pool_passed = m.counter("dve_passed"), m.counter("pool_passed")
        s_stats = m.counter("s_stats", 8)
        s_aggr = m.counter("s_aggr", 8)
        s_seed = m.counter("s_seed", 2 * SEED)
        s_rstd = m.counter("s_rstd", 2 * NEWTON)
        s_norm0 = m.counter("s_norm0", 4)
        s_h = m.counter("s_h", 2)
        s_norm1 = m.counter("s_norm1", 4)
        h_kept = m.counter("h_kept", 16)
        xT_mm = m.counter("xT_mm", 2)
        xT_f = m.counter("xT_f", 2)
        xT_hi = m.counter("xT_hi", 2)
        xT_lo = m.counter("xT_lo", 2)
        q_mm = m.counter("q_mm", 2)
        q_hi = m.counter("q_hi", 4)
        q_lo = m.counter("q_lo", 4)
        k_mm = m.counter("k_mm", 2)
        k_hi = m.counter("k_hi", 2)
        k_lo = m.counter("k_lo", 2)
        k_spread = m.counter("k_spread", 64)
        v_mm = m.counter("v_mm", 4)
        v_sb = m.counter("v_sb", 4)
        drive_mm = m.counter("drive_mm", 1)
        drive_sb = m.counter("drive_sb", 1)
        scanned = m.counter("scanned", 1)
        st_hi = m.counter("st_hi", 1)
        st_lo = m.counter("st_lo", 1)
        q_scores = m.counter("q_scores", 2 * NW)
        maxed = m.counter("maxed", 2 * NW)
        maxT_mm = m.counter("maxT_mm", NW)
        maxT_sb = m.counter("maxT_sb", NW)
        k_scores = m.counter("k_scores", NW)
        exped = m.counter("exped", NW)
        pv_mm = m.counter("pv_mm", NW)
        recip = m.counter("recip", NW)
        o_norm = m.counter("o_norm", 2 * NW)
        oT_mm = m.counter("oT_mm", NW)
        oT_hi = m.counter("oT_hi", NW)
        oT_lo = m.counter("oT_lo", NW)
        gate_mm = m.counter("gate_mm", TT)
        y_mm = m.counter("y_mm", TT)
        gate_sb = m.counter("gate_sb", TT)
        gated = m.counter("gated", TT)
        mixed = m.counter("mixed", TT)
        x1_sb = m.counter("x1_sb", TT)
        x1_out = m.counter("x1_out", 16)
        block = ctx.enter_context(nc.Block())
        pvO = pv[:, 0:PAIRS * (2 * DH + 1)].rearrange("p (a d) -> p a d", a=PAIRS)
        steps = range(NW + 3)

        def by_window(ap):
            return ap.rearrange("p (n q) -> p n q", n=NW)

        def loop(eng, body):
            body(0, False)
            with eng.Fori(1, NB - 1) as b:
                body(b, False)
            body(NB - 1, True)

        @block.sync
        def _(sp):
            def load(b):
                sp.dma_start(x[:], din["x"][bass.ds(b, 1), :, :].rearrange("a (t p) d -> p (a t) d", p=P)
                             ).then_inc(x_in.sem, 16)
                row = scratch["mod"][bass.ds(b, 1), 0:2 * D].rearrange("a (i d) -> a i d", i=2)
                sp.dma_start(shsc[:], row.to_broadcast([P, 2, D])).then_inc(x_in.sem, 16)

            def body(b, last):
                sp.wait_ge(k_lo.sem, k_lo.at(b, 2))
                for j in range(4):
                    r = slice(32 * j, 32 * j + 32)
                    sp.dma_start(Kz[r, j, :, :, WIN:], Kt[r, :, :, :]).then_inc(k_spread.sem, 16)
                if not last:
                    sp.wait_ge(s_norm0.sem, s_norm0.at(b, 4))
                    sp.wait_ge(s_h.sem, s_h.at(b, 2))
                    load(b + 1)
                sp.wait_ge(s_h.sem, s_h.at(b, 2))
                sp.wait_ge(x1_sb.sem, x1_sb.at(b, 0))
                sp.dma_start(hres[:], h[:]).then_inc(h_kept.sem, 16)
                sp.wait_ge(x1_sb.sem, x1_sb.at(b, TT))
                sp.dma_start(scratch["x1"][bass.ds(b, 1), :, :].rearrange("a (t p) d -> p (a t) d", p=P),
                             x1[:]).then_inc(x1_out.sem, 16)

            load(0)
            loop(sp, body)
            sp.wait_ge(x1_out.sem, 16 * NB)

        @block.tensor
        def _(pe):
            def transpose_x(b):
                pe.wait_ge(s_norm1.sem, s_norm1.at(b, 4))
                pe.wait_ge(oT_lo.sem, oT_lo.at(b, 0))
                for k in range(KD):
                    for t in range(TT):
                        last = pe.transpose(pj[:, k, t * P:(t + 1) * P], nrm[:, t, k * P:(k + 1) * P],
                                            w["identf"][:])
                    last.then_inc(xT_mm.sem, 1)

            def columns(out, weight, c, done):
                for k in range(KD):
                    last = hi_lo_products(pe, out, [a[:, k, c:c + P] for a in weight],
                                          [a[:, k, WIN:] for a in (xTh, xTl)], k == 0, k == KD - 1)
                last.then_inc(done.sem, 1)

            def value_rows(u):
                for i in range(2):
                    t0 = WIN * (2 * u + i)
                    for k in range(KD):
                        last = hi_lo_products(pe, v_bank[u][:, i * D:(i + 1) * D],
                                              [a[:, k, t0:t0 + P] for a in (xTh, xTl)],
                                              [a[:, k, :] for a in w["v"]], k == 0, k == KD - 1)
                last.then_inc(v_mm.sem, 1)

            def project(b):
                pe.wait_ge(xT_lo.sem, xT_lo.at(b, 2))
                for c in range(2):
                    columns(q_bank[c], w["qk"], c * P, q_mm)
                pe.wait_ge(gated.sem, gated.at(b, 0))
                for c in range(2):
                    columns(k_bank[c], w["qk"], (2 + c) * P, k_mm)
                columns(drive_bank, w["drive"], 0, drive_mm)
                value_rows(0)
                for u in (1, 2):
                    pe.wait_ge(q_lo.sem, q_lo.at(b, 2 * u))
                    value_rows(u)

            def scores_by_query(b, n):
                var = 1 if n == 0 else 0
                for c in range(2):
                    if n == 0:
                        pe.wait_ge(k_lo.sem, k_lo.at(b, c + 1))
                    else:
                        pe.wait_ge(maxed.sem, maxed.at(b, 2 * n - 1 + c))
                    pe.matmul(sc[:, c, :], w["twoI"][:], w["maskq"][:, var, :, :], start=True, stop=False)
                    for j in range(4):
                        last = pe.matmul(sc[:, c, j * P:(j + 1) * P],
                                         Qh[:, c, n, :, :].rearrange("p a q -> p (a q)"),
                                         Kz[:, j, 0, c, WIN * n:WIN * n + P], start=False, stop=(j == 3))
                    last.then_inc(q_scores.sem, 1)

            def scores_by_key(b, n):
                pe.wait_ge(maxT_sb.sem, maxT_sb.at(b, n + 1))
                if n > 0:
                    pe.wait_ge(exped.sem, exped.at(b, n))
                var = 1 if n == 0 else 0
                for c in range(2):
                    q = [a[:, c, n, :, :].rearrange("p a q -> p (a q)") for a in (Qh, Ql)]
                    for j in range(4):
                        out = sc[:, 2 + c, j * P:(j + 1) * P]
                        pe.matmul(out, w["select"][:, var, 4 * c + j, :], w["shift"][:, n % 2, :],
                                  start=True, stop=False)
                        last = hi_lo_products(pe, out, [Kz[:, j, i, c, WIN * n:WIN * n + P] for i in range(2)],
                                              q, False, True)
                last.then_inc(k_scores.sem, 1)

            def values(b, n):
                pe.wait_ge(exped.sem, exped.at(b, n + 1))
                if n > 0:
                    pe.wait_ge(o_norm.sem, o_norm.at(b, 2 * n))
                for i in range(PAIRS):
                    last = pe.matmul(pvO[:, i, :], prob[:, n % 2, i * P:(i + 1) * P], V[:, n, i, :],
                                     start=True, stop=True)
                last.then_inc(pv_mm.sem, 1)

            def gate_and_attention(b, t):
                pe.wait_ge(oT_lo.sem, oT_lo.at(b, 2 * t + 2))
                if t == 0:
                    pe.wait_ge(st_lo.sem, st_lo.at(b, 1))
                tok = slice(t * P, (t + 1) * P)
                for k in range(KD):
                    hi_lo_products(pe, sc[:, t, 0:D], [a[:, k, WIN + t * P:WIN + (t + 1) * P] for a in (xTh, xTl)],
                                   [a[:, k, :] for a in w["g"]], k == 0, False)
                pe.matmul(sc[:, t, 0:D], w["ones3"][:], w["bg3"][:], start=False, stop=True)
                for par in range(2):
                    hi_lo_products(pe, sc[:, t, D:], [a[:, par, tok] for a in (oTh, oTl)],
                                   [a[:, par, :] for a in w["o"]], par == 0, False)
                hi_lo_products(pe, sc[:, t, D:], [sth[:, tok], stl[:, tok]], [a[:, 0, :] for a in w["nc"]],
                               False, False)
                pe.matmul(sc[:, t, D:], w["ones3"][:], w["bo3"][:], start=False, stop=True).then_inc(gate_mm.sem, 1)

            def recurrence_out(b, t):
                tok = slice(t * P, (t + 1) * P)
                if t == 0:
                    pe.wait_ge(maxT_sb.sem, maxT_sb.at(b, NW))
                elif t == 1:
                    pe.wait_ge(o_norm.sem, o_norm.at(b, 2 * NW))
                else:
                    pe.wait_ge(mixed.sem, mixed.at(b, t - 1))
                hi_lo_products(pe, y_bank[t % 2], [sth[:, tok], stl[:, tok]],
                               [a[:, 0, :] for a in w["c"]], True, True).then_inc(y_mm.sem, 1)

            def body(b, last):
                project(b)
                for s in steps:
                    if s == 0:
                        pe.wait_ge(k_spread.sem, k_spread.at(b, 64))
                    if s < NW:
                        scores_by_query(b, s)
                    if s == 0:
                        pe.wait_ge(drive_sb.sem, drive_sb.at(b, 1))
                        value_rows(3)
                        pe.wait_ge(mixed.sem, mixed.at(b, 0))
                    if s == NW:
                        gate_and_attention(b, 0)
                    if s == NW + 1:
                        gate_and_attention(b, 1)
                    if s == 1:
                        pe.wait_ge(v_sb.sem, v_sb.at(b, 4))
                    if 0 <= s - 1 < NW:
                        scores_by_key(b, s - 1)
                    if 0 <= s - 2 < NW:
                        values(b, s - 2)
                    if s < NW:
                        pe.wait_ge(maxed.sem, maxed.at(b, 2 * s + 2))
                        pe.transpose(maxT, mx[:, s % 2, :], w["identb"][:]).then_inc(maxT_mm.sem, 1)
                    if 0 <= s - 3 < NW:
                        n = s - 3
                        pe.wait_ge(o_norm.sem, o_norm.at(b, 2 * n + 2))
                        if n >= 2:
                            pe.wait_ge(oT_lo.sem, oT_lo.at(b, n - 1))
                        pe.transpose(pj[:, n % 2, 0:P], on[:, n % 2, :, :], w["identf"][:]).then_inc(oT_mm.sem, 1)
                    if s == NW + 1:
                        gate_and_attention(b, 2)
                recurrence_out(b, 0)
                recurrence_out(b, 1)
                gate_and_attention(b, 3)
                if not last:
                    transpose_x(b + 1)
                recurrence_out(b, 2)
                recurrence_out(b, 3)

            transpose_x(0)
            loop(pe, body)

        @block.scalar
        def _(act):
            def affine(b):
                for k in range(KD):
                    act.wait_ge(xT_mm.sem, xT_mm.at(b, k + 1))
                    if k == 0:
                        act.wait_ge(xT_lo.sem, xT_lo.at(b, 0))
                    act.activation(xTf[:, k, :], pj[:, k, :], ACT.Identity, bias=w["b1"][:, k:k + 1],
                                   scale=w["g1"][:, k:k + 1]).then_inc(xT_f.sem, 1)

            def body(b, last):
                for c in range(2):
                    act.wait_ge(q_mm.sem, q_mm.at(b, c + 1))
                    for par in range(2):
                        act.mul(Qh[:, c, :, par, :], by_window(q_bank[c]), w["parity"][:, par:par + 1]
                                ).then_inc(q_hi.sem, 1)
                for c in range(2):
                    act.wait_ge(k_mm.sem, k_mm.at(b, c + 1))
                    act.copy(Kt[:, 0, c, :], k_bank[c]).then_inc(k_hi.sem, 1)
                act.wait_ge(drive_mm.sem, drive_mm.at(b, 1))
                act.wait_ge(scanned.sem, scanned.at(b, 0))
                act.activation(drv[:], drive_bank, ACT.Identity, bias=w["bu"][:, 0:1]).then_inc(drive_sb.sem, 1)
                for u in range(4):
                    act.wait_ge(v_mm.sem, v_mm.at(b, u + 1))
                    act.copy(V[:, 2 * u:2 * u + 2, :, 0:2 * DH],
                             v_bank[u].rearrange("p (n a d) -> p n a d", n=2, a=PAIRS)
                             ).then_inc(v_sb.sem, 1)
                for s in steps:
                    if 0 <= s - 1 < NW:
                        n = s - 1
                        act.wait_ge(k_scores.sem, k_scores.at(b, n + 1))
                        act.activation(prob[:, n % 2, :].rearrange("p (c j) -> p c j", c=2), sc[:, 2:4, :],
                                       ACT.Exp, scale=SCALE).then_inc(exped.sem, 1)
                    if 0 <= s - 3 < NW:
                        n = s - 3
                        act.wait_ge(oT_mm.sem, oT_mm.at(b, n + 1))
                        act.copy(oTh[:, :, WIN * n:WIN * n + WIN],
                                 pj[:, n % 2, 0:P].rearrange("p (a q) -> p a q", a=2)).then_inc(oT_hi.sem, 1)
                for t in range(TT):
                    act.wait_ge(gate_mm.sem, gate_mm.at(b, t + 1))
                    if t == 0:
                        act.wait_ge(x1_sb.sem, x1_sb.at(b, 0))
                    act.activation(mix[:, t, :], sc[:, t, 0:D], ACT.Tanh, scale=0.5).then_inc(gate_sb.sem, 1)
                if not last:
                    affine(b + 1)

            affine(0)
            loop(act, body)

        def moments(dve, b, src, half):
            for t in range(TT):
                dve.bn_stats(stats[:, t, :], src[:, t, :]).then_inc(s_stats.sem, 1)

        def aggregate(dve, b, half):
            wait_alone(dve, s_stats.sem, s_stats.at(b, 4 * half + 4), dve_passed)
            for t in range(TT):
                dve.bn_aggr(mv[:, t, :], stats[:, t, :]).then_inc(s_aggr.sem, 1)
            dve.wait_ge(s_aggr.sem, s_aggr.at(b, 4 * half + 4))
            seed_inverse_root(dve, s_seed, b, SEED * half, mv[:, :, 1], ve[:], rs[:])

        def normalize(dve, b, src, half, done):
            dve.wait_ge(s_rstd.sem, s_rstd.at(b, NEWTON * (half + 1)))
            for t in range(TT):
                dve.tensor_scalar(nrm[:, t, :], src[:, t, :], mv[:, t, 0:1], rs[:, t:t + 1], ALU.subtract,
                                  ALU.mult).then_inc(done.sem, 1)

        def layer_norms(dve, b, part):
            if part == 0:
                dve.wait_ge(x_in.sem, x_in.at(b, 32))
                moments(dve, b, x, 0)
            if part == 1:
                aggregate(dve, b, 0)
            if part == 2:
                dve.wait_ge(xT_mm.sem, xT_mm.at(b, 0))
                normalize(dve, b, x, 0, s_norm0)
            if part == 5:
                dve.wait_ge(s_h.sem, s_h.at(b, 2))
                moments(dve, b, h, 1)
            if part == 6:
                aggregate(dve, b, 1)
            if part == 7:
                normalize(dve, b, h, 1, s_norm1)

        @block.vector
        def _(dve):
            def split_x(b):
                dve.wait_ge(gate_mm.sem, gate_mm.at(b, 0))
                for k in range(KD):
                    dve.wait_ge(xT_f.sem, xT_f.at(b, k + 1))
                    dve.tensor_copy(xTh[:, k, WIN:], xTf[:, k, :]).then_inc(xT_hi.sem, 1)
                for k in range(KD):
                    dve.wait_ge(xT_hi.sem, xT_hi.at(b, k + 1))
                    dve.tensor_tensor(xTl[:, k, WIN:], xTf[:, k, :], xTh[:, k, WIN:], ALU.subtract
                                      ).then_inc(xT_lo.sem, 1)

            def body(b, last):
                for c in range(2):
                    dve.wait_ge(q_hi.sem, q_hi.at(b, 2 * c + 2))
                    for par in range(2):
                        dve.scalar_tensor_tensor(out=Ql[:, c, :, par, :], in0=by_window(q_bank[c]),
                                                 scalar=w["parity"][:, par:par + 1], in1=Qh[:, c, :, par, :],
                                                 op0=ALU.mult, op1=ALU.subtract).then_inc(q_lo.sem, 1)
                for c in range(2):
                    dve.wait_ge(k_hi.sem, k_hi.at(b, c + 1))
                    dve.tensor_tensor(Kt[:, 1, c, :], k_bank[c], Kt[:, 0, c, :], ALU.subtract
                                      ).then_inc(k_lo.sem, 1)
                for s in steps:
                    if s < NW:
                        for c in range(2):
                            dve.wait_ge(q_scores.sem, q_scores.at(b, 2 * s + c + 1))
                            dve.tensor_reduce(mx[:, s % 2, WIN + 4 * c:WIN + 4 * c + 4],
                                              sc[:, c, :].rearrange("p (j k) -> p j k", j=4),
                                              AX.X, ALU.max).then_inc(maxed.sem, 1)
                    if s == 1:
                        dve.wait_ge(drive_sb.sem, drive_sb.at(b, 1))
                        dve.wait_ge(st_lo.sem, st_lo.at(b, 0))
                        dve.tensor_tensor_scan(st[:], w["A"][:, 0:1].to_broadcast([P, L]), drv[:], 0.0, ALU.mult,
                                               ALU.add).then_inc(scanned.sem, 1)
                        dve.wait_ge(scanned.sem, scanned.at(b, 1))
                        dve.tensor_copy(sth[:], st[:]).then_inc(st_hi.sem, 1)
                    if not last:
                        layer_norms(dve, b + 1, s)
                    if 0 <= s - 2 < NW:
                        n = s - 2
                        dve.wait_ge(pv_mm.sem, pv_mm.at(b, n + 1))
                        dve.reciprocal(rden[:, n % 2, :], pvO[:, :, 2 * DH]).then_inc(recip.sem, 1)
                        dve.wait_ge(recip.sem, recip.at(b, n + 1))
                        for par in range(2):
                            r = slice(WIN * par, WIN * par + WIN)
                            dve.tensor_tensor(on[r, n % 2, :, :], pvO[r, :, DH * par:DH * par + DH],
                                              rden[r, n % 2, :].unsqueeze(2).to_broadcast([WIN, PAIRS, DH]),
                                              ALU.mult).then_inc(o_norm.sem, 1)
                    if s < NW:
                        dve.wait_ge(maxT_mm.sem, maxT_mm.at(b, s + 1))
                        dve.tensor_copy(w["shift"][WIN:WIN + PAIRS, s % 2, :], maxT[WIN:WIN + PAIRS, :]
                                        ).then_inc(maxT_sb.sem, 1)
                    if 0 <= s - 3 < NW:
                        n = s - 3
                        dve.wait_ge(oT_hi.sem, oT_hi.at(b, n + 1))
                        dve.tensor_tensor(oTl[:, :, WIN * n:WIN * n + WIN],
                                          pj[:, n % 2, 0:P].rearrange("p (a q) -> p a q", a=2),
                                          oTh[:, :, WIN * n:WIN * n + WIN], ALU.subtract).then_inc(oT_lo.sem, 1)
                for t in range(TT):
                    dve.wait_ge(gate_sb.sem, gate_sb.at(b, t + 1))
                    dve.scalar_tensor_tensor(out=mix[:, t, :], in0=mix[:, t, :], scalar=1.0, in1=sc[:, t, D:],
                                             op0=ALU.add, op1=ALU.mult).then_inc(gated.sem, 1)
                    dve.wait_ge(gated.sem, gated.at(b, t + 1))
                    dve.wait_ge(y_mm.sem, y_mm.at(b, t + 1))
                    dve.scalar_tensor_tensor(out=mix[:, t, :], in0=mix[:, t, :], scalar=0.5,
                                             in1=y_bank[t % 2], op0=ALU.mult, op1=ALU.add
                                             ).then_inc(mixed.sem, 1)
                if not last:
                    split_x(b + 1)

            for part in range(8):
                layer_norms(dve, 0, part)
            split_x(0)
            loop(dve, body)

        @block.gpsimd
        def _(pool):
            def inverse_deviation(b, half):
                pool.wait_ge(s_seed.sem, s_seed.at(b, SEED * (half + 1)))
                refine_inverse_root(pool, s_rstd, b, NEWTON * half, ve[:], rs[:], nt[:], pool_passed)

            def modulate(b):
                inverse_deviation(b, 0)
                pool.wait_ge(s_norm0.sem, s_norm0.at(b, 4))
                pool.wait_ge(h_kept.sem, h_kept.at(b, 0))
                pool.tensor_tensor(h[:], nrm[:], shsc[:, 1:2, :].to_broadcast([P, TT, D]), ALU.mult
                                   ).then_inc(s_h.sem, 1)
                pool.wait_ge(s_h.sem, s_h.at(b, 1))
                pool.tensor_tensor(h[:], h[:], shsc[:, 0:1, :].to_broadcast([P, TT, D]), ALU.add
                                   ).then_inc(s_h.sem, 1)
                inverse_deviation(b, 1)

            def body(b, last):
                pool.wait_ge(st_hi.sem, st_hi.at(b, 1))
                pool.tensor_tensor(stl[:], st[:], sth[:], ALU.subtract).then_inc(st_lo.sem, 1)
                if not last:
                    modulate(b + 1)
                pool.wait_ge(h_kept.sem, h_kept.at(b, 16))
                pool.wait_ge(x1_out.sem, x1_out.at(b, 0))
                for t in range(TT):
                    pool.wait_ge(mixed.sem, mixed.at(b, t + 1))
                    pool.tensor_tensor(x1[:, t, :], mix[:, t, :], hres[:, t, :], ALU.add).then_inc(x1_sb.sem, 1)

            modulate(0)
            loop(pool, body)



ROUTE = 19
HB = 4
POOLED = (0, 1, 2)


def mlp(nc, din, w, x_w, scratch, NB, keep, capacity):
    assert NB <= 2 * E
    with ExitStack() as ctx:
        m = Memory(nc, ctx, "mlp_")
        xa = m.sb("xa", [P, TT, D])
        xb = m.sb("xb", [P, TT, D])
        x = m.sb("x", [P, TT, D])
        ga = m.sb("ga", [P, 1, D])
        shsc = m.sb("shsc", [P, 2, D])
        nrm = m.sb("nrm", [P, TT, D])
        stats = m.sb("stats", [P, 2, TT, 6])
        mv = m.sb("mv", [P, 2, TT, 2])
        ve, rs, nt = (m.sb(n, [P, 2, TT]) for n in ("ve", "rs", "nt"))
        xTf = m.sb("xTf", [P, KD, L])
        xT = [m.sb(n, [P, KD, L], F16) for n in ("xTh", "xTl")]
        hid = m.sb("hid", [P, HB, L])
        hd = [m.sb(n, [P, FMC, L], F16) for n in ("hidh", "hidl")]
        stage = m.sb("stage", [P, PIECE])
        piece = expert_pieces(din, x_w, stage)
        x2 = m.sb("x2", [P, TT, D])
        h2 = m.sb("h2", [P, TT, D])
        rows = m.sb("rows", [P, TT, 2, D], F16)
        hT = m.sb("hT", [P, TT, 4, P], F16)
        lg = m.sb("lg", [P, TT, E])
        srt = m.sb("srt", [P, TT, 8])
        ix = m.sb("ix", [P, TT, 8], U32)
        ixf = m.sb("ixf", [P, TT * 2])
        oh = m.sb("oh", [P, TT * 2, E])
        mem = m.sb("mem", [P, TT, E], BF16)
        pos = m.sb("pos", [P, TT, E])
        picked = m.sb("picked", [P, TT * 2, E])
        slotf = m.sb("slotf", [P, TT * 2])
        slot = m.sb("slot", [P, TT * 2], I32)
        iota8 = m.sb("iota8", [P, E])
        pj = m.ps("pj", [P, 2, 512])
        po = m.ps("po", [P, 2, 512])
        pt = m.ps("pt", [P, 2, 1024], F16)
        pg = m.ps("pg", [P, 512])
        pp = m.ps("pp", [P, 512])
        base = keep["base"]

        xa_in = m.counter("xa_in", 16)
        xb_in = m.counter("xb_in", 48)
        sh_in = m.counter("sh_in", 16)
        dve_passed, pool_passed = m.counter("dve_passed"), m.counter("pool_passed")
        s_stats, s_aggr = m.counter("s_stats", 4), m.counter("s_aggr", 4)
        root = m.counter("root", ROOT)
        s_norm = m.counter("s_norm", 4)
        t_stats, t_aggr = m.counter("t_stats", 4), m.counter("t_aggr", 4)
        t_norm = m.counter("t_norm", 4)
        xT_mm, xT_f = m.counter("xT_mm", 2), m.counter("xT_f", 2)
        xT_hi, xT_lo = m.counter("xT_hi", 2), m.counter("xT_lo", 2)
        hid_mm, hid_f = m.counter("hid_mm", FMC), m.counter("hid_f", FMC)
        hid_hi, hid_lo = m.counter("hid_hi", FMC), m.counter("hid_lo", FMC - len(POOLED))
        hid_lo_pool = m.counter("hid_lo_pool", len(POOLED))
        out_mm = m.counter("out_mm", TT)
        out_sb = m.counter("out_sb", TT)
        x2_sb = m.counter("x2_sb", TT)
        piece_in, piece_hi, piece_lo = m.counter("piece_in", 32), m.counter("piece_hi", 2), m.counter("piece_lo", 2)
        x2_gated = m.counter("x2_gated", TT)
        x2_out = m.counter("x2_out", 16)
        s_h2 = m.counter("s_h2", 2)
        row_hi, row_lo = m.counter("row_hi", 1), m.counter("row_lo", 1)
        hT_mm, hT_sb = m.counter("hT_mm", 2), m.counter("hT_sb", 2)
        gate_mm = m.counter("gate_mm", 1)
        prefix_mm = m.counter("prefix_mm", 1)
        route = m.counter("route", ROUTE)
        sent = m.counter("sent", 16 * 2 * TT)
        ready = m.counter("ready", 1)
        block = ctx.enter_context(nc.Block())

        def loop(eng, body):
            body(0, False, False, False)
            body(1, True, False, False)
            with eng.Fori(2, NB - 1) as b:
                body(b, True, True, False)
            body(NB - 1, True, True, True)


        def low_done(eng, b, c):
            if c < 0:
                b, c = b - 1, c + FMC
            on_pool = len([q for q in POOLED if q <= c])
            sig, n = (hid_lo_pool, on_pool) if c in POOLED else (hid_lo, c + 1 - on_pool)
            eng.wait_ge(sig.sem, sig.at(b, n))

        def rows_of(ap, b):
            return ap[bass.ds(b, 1), :, :].rearrange("a (t p) d -> p (a t) d", p=P)

        @block.sync
        def _(sp):
            def load_x1(b):
                sp.dma_start(xa[:], rows_of(scratch["x1"], b)).then_inc(xa_in.sem, 16)

            def body(b, second, third, last):
                if not last:
                    sp.wait_ge(s_norm.sem, s_norm.at(b + 1, 0))
                    load_x1(b + 1)
                sp.wait_ge(piece_lo.sem, piece_lo.at(b, 0))
                for src, area, _ in piece(b):
                    sp.dma_start(area, src).then_inc(piece_in.sem, 16)
                sp.wait_ge(x2_sb.sem, x2_sb.at(b, 0))
                sp.dma_start(xb[:], rows_of(scratch["x1"], b)).then_inc(xb_in.sem, 16)
                sp.dma_start(x[:], rows_of(din["x"], b)).then_inc(xb_in.sem, 16)
                sp.dma_start(ga[:], scratch["mod"][bass.ds(b, 1), 2 * D:3 * D].rearrange("a (i d) -> a i d", i=1)
                             .to_broadcast([P, 1, D])).then_inc(xb_in.sem, 16)
                sp.wait_ge(s_h2.sem, s_h2.at(b, 0))
                sp.dma_start(shsc[:], scratch["mod"][bass.ds(b, 1), 3 * D:5 * D]
                             .rearrange("a (i d) -> a i d", i=2).to_broadcast([P, 2, D])).then_inc(sh_in.sem, 16)

            load_x1(0)
            loop(sp, body)

        @block.tensor
        def _(pe):
            def transpose_x(b):
                for k in range(KD):
                    if k == 0:
                        pe.wait_ge(s_norm.sem, s_norm.at(b, 4))
                        pe.wait_ge(hid_f.sem, hid_f.at(b, 0))
                    for t in range(TT):
                        last = pe.transpose(pj[:, k, t * P:(t + 1) * P], nrm[:, t, k * P:(k + 1) * P],
                                            w["identf"][:])
                    last.then_inc(xT_mm.sem, 1)

            def hidden(b, c):
                if c == 0:
                    pe.wait_ge(xT_lo.sem, xT_lo.at(b, 2))
                if c >= 2:
                    pe.wait_ge(hid_f.sem, hid_f.at(b, c - 1))
                for k in range(KD):
                    last = hi_lo_products(pe, pj[:, c % 2, :], [a[:, k, c * P:(c + 1) * P] for a in w["w1"]],
                                          [a[:, k, :] for a in xT], k == 0, k == KD - 1)
                last.then_inc(hid_mm.sem, 1)

            def project(b, t):
                if t >= 2:
                    pe.wait_ge(out_sb.sem, out_sb.at(b, t - 1))
                else:
                    pe.wait_ge(out_sb.sem, out_sb.at(b, 0))
                for c in range(FMC):
                    if t == 0:
                        low_done(pe, b, c)
                    hi_lo_products(pe, po[:, t % 2, 0:D], [a[:, c, t * P:(t + 1) * P] for a in hd],
                                   [a[:, c, :] for a in w["w2"]], c == 0, False)
                pe.matmul(po[:, t % 2, 0:D], w["ones3"][:], w["b23"][:], start=False, stop=True
                          ).then_inc(out_mm.sem, 1)

            def transpose_rows(a):
                pe.wait_ge(row_lo.sem, row_lo.at(a, 1))
                for u in range(2):
                    for t in (2 * u, 2 * u + 1):
                        for i in range(2):
                            for k in range(KD):
                                at = ((t % 2) * 4 + i * 2 + k) * P
                                last = pe.transpose(pt[:, u, at:at + P], rows[:, t, i, k * P:(k + 1) * P],
                                                    w["identh"][:])
                    last.then_inc(hT_mm.sem, 1)

            def gate(a):
                pe.wait_ge(hT_sb.sem, hT_sb.at(a, 2))
                for t in range(TT):
                    for k in range(KD):
                        last = hi_lo_products(pe, pg[:, t * E:(t + 1) * E], [hT[:, t, i * 2 + k, :] for i in range(2)],
                                              [g[:, k, :] for g in w["gate"]], k == 0, k == KD - 1)
                last.then_inc(gate_mm.sem, 1)

            def prefix(a):
                pe.wait_ge(route.sem, route.at(a, 12))
                flat = mem[:].rearrange("p t e -> p (t e)")
                pe.matmul(pp[:, 0:TT * E], w["before"][:], flat, start=True, stop=False)
                for t in range(1, TT):
                    pe.matmul(pp[:, t * E:TT * E], w["ones"][:], flat[:, 0:(TT - t) * E], start=False,
                              stop=(t == TT - 1))
                for t in range(TT):
                    last = pe.matmul(pp[:, TT * E:TT * E + E], w["ones"][:], mem[:, t, :], start=(t == 0),
                                     stop=(t == TT - 1))
                last.then_inc(prefix_mm.sem, 1)

            def body(b, second, third, last):
                for c in range(FMC):
                    hidden(b, c)
                    if third and c == 1:
                        transpose_rows(b - 2)
                if third:
                    gate(b - 2)
                if not last:
                    transpose_x(b + 1)
                for t in range(TT):
                    project(b, t)
                    if third and t == 0:
                        prefix(b - 2)

            transpose_x(0)
            loop(pe, body)
            for a in (NB - 2, NB - 1):
                transpose_rows(a)
                gate(a)
                prefix(a)

        @block.scalar
        def _(act):
            def copy_rows(a):
                for u in range(2):
                    act.wait_ge(hT_mm.sem, hT_mm.at(a, u + 1))
                    act.copy(hT[:, 2 * u:2 * u + 2, :, :].rearrange("p t i q -> p (t i q)"), pt[:, u, :]
                             ).then_inc(hT_sb.sem, 1)

            def x_parts(b):
                for k in range(KD):
                    act.wait_ge(xT_mm.sem, xT_mm.at(b, k + 1))
                    act.activation(xTf[:, k, :], pj[:, k, :], ACT.Identity, bias=w["b2"][:, k:k + 1],
                                   scale=w["g2"][:, k:k + 1]).then_inc(xT_f.sem, 1)
                for k in range(KD):
                    act.wait_ge(xT_f.sem, xT_f.at(b, k + 1))
                    act.copy(xT[0][:, k, :], xTf[:, k, :]).then_inc(xT_hi.sem, 1)

            def store_x2(b):
                act.wait_ge(x2_sb.sem, x2_sb.at(b + 1, 0))
                act.dma_start(rows_of(scratch["x2"], b), x2[:]).then_inc(x2_out.sem, 16)

            def body(b, second, third, last):
                for c in range(FMC + 1):
                    if second and c == 2:
                        store_x2(b - 1)
                    if c < FMC:
                        act.wait_ge(hid_mm.sem, hid_mm.at(b, c + 1))
                        low_done(act, b, c - HB)
                        act.activation(hid[:, c % HB, :], pj[:, c % 2, :], ACT.Gelu, bias=w["mb1"][:, c:c + 1]
                                       ).then_inc(hid_f.sem, 1)
                    if c > 0:
                        act.wait_ge(hid_f.sem, hid_f.at(b, c))
                        act.copy(hd[0][:, c - 1, :], hid[:, (c - 1) % HB, :]).then_inc(hid_hi.sem, 1)
                    if third and c == 2:
                        copy_rows(b - 2)
                if not last:
                    x_parts(b + 1)
                act.wait_ge(piece_in.sem, piece_in.at(b, 32))
                for _, area, places in piece(b):
                    act.copy(places[0], area).then_inc(piece_hi.sem, 1)

            x_parts(0)
            loop(act, body)
            store_x2(NB - 1)
            copy_rows(NB - 2)
            copy_rows(NB - 1)
            act.wait_ge(x2_out.sem, 16 * NB)

        @block.vector
        def _(dve):
            def deviations(passed, of_x1, of_x2):
                sets = [(0, of_x1, xa, s_stats, s_aggr, s_norm), (1, of_x2, x2, t_stats, t_aggr, t_norm)]
                sets = [one for one in sets if one[1] is not None]
                for i, b, src, sig_st, _, _ in sets:
                    if i == 0:
                        dve.wait_ge(xa_in.sem, xa_in.at(b, 16))
                    else:
                        dve.wait_ge(x2_sb.sem, x2_sb.at(b, TT))
                    for t in range(TT):
                        dve.bn_stats(stats[:, i, t, :], src[:, t, :]).then_inc(sig_st.sem, 1)
                for i, b, _, sig_st, sig_ag, sig_norm in sets:
                    dve.wait_ge(sig_norm.sem, sig_norm.at(b, 0))
                    wait_alone(dve, sig_st.sem, sig_st.at(b, 4), dve_passed)
                    for t in range(TT):
                        dve.bn_aggr(mv[:, i, t, :], stats[:, i, t, :]).then_inc(sig_ag.sem, 1)
                for _, b, _, _, sig_ag, _ in sets:
                    dve.wait_ge(sig_ag.sem, sig_ag.at(b, 4))
                k = slice(sets[0][0], sets[-1][0] + 1)
                inverse_root(dve, root, passed, mv[:, k, :, 1], ve[:, k, :], rs[:, k, :], nt[:, k, :])

            def norm_x1(b):
                dve.wait_ge(xT_mm.sem, xT_mm.at(b, 0))
                for t in range(TT):
                    dve.tensor_scalar(nrm[:, t, :], xa[:, t, :], mv[:, 0, t, 0:1], rs[:, 0, t:t + 1], ALU.subtract,
                                      ALU.mult).then_inc(s_norm.sem, 1)

            def norm_x2(a):
                dve.wait_ge(row_lo.sem, row_lo.at(a, 0))
                for t in range(TT):
                    dve.tensor_scalar(h2[:, t, :], x2[:, t, :], mv[:, 1, t, 0:1], rs[:, 1, t:t + 1], ALU.subtract,
                                      ALU.mult).then_inc(t_norm.sem, 1)

            def split_rows(a):
                dve.wait_ge(s_h2.sem, s_h2.at(a, 2))
                dve.wait_ge(sent.sem, sent.at(a, 0))
                dve.wait_ge(hT_mm.sem, hT_mm.at(a, 0))
                dve.tensor_copy(rows[:, :, 0, :], h2[:]).then_inc(row_hi.sem, 1)
                dve.wait_ge(row_hi.sem, row_hi.at(a, 1))
                dve.tensor_tensor(rows[:, :, 1, :], h2[:], rows[:, :, 0, :], ALU.subtract).then_inc(row_lo.sem, 1)

            def choose(a):
                n = 0

                def step(ins, wait=True):
                    nonlocal n
                    ins.then_inc(route.sem, 1)
                    n += 1
                    if wait:
                        wait_alone(dve, route.sem, route.at(a, n), dve_passed)

                dve.wait_ge(gate_mm.sem, gate_mm.at(a, 1))
                step(dve.tensor_copy(lg[:].rearrange("p t e -> p (t e)"), pg[:, 0:TT * E]))
                for t in range(TT):
                    step(dve.max(srt[:, t, :], lg[:, t, :]), t == TT - 1)
                for t in range(TT):
                    step(dve.max_index(ix[:, t, :], srt[:, t, :], lg[:, t, :]), t == TT - 1)
                step(dve.tensor_copy(ixf[:].rearrange("p (t k) -> p t k", k=2), ix[:, :, 0:2]))
                step(dve.tensor_tensor(oh[:], iota8[:].unsqueeze(1).to_broadcast([P, 2 * TT, E]),
                                       ixf[:].unsqueeze(2).to_broadcast([P, 2 * TT, E]), ALU.is_equal))
                both = oh[:].rearrange("p (t k) e -> p t k e", k=2)
                step(dve.tensor_tensor(mem[:], both[:, :, 0, :], both[:, :, 1, :], ALU.add))
                step(dve.tensor_copy(keep["top"][:, bass.ds(a * TT, TT), :], srt[:, :, 0:2]), False)
                return n

            def place(a):
                n = 13
                dve.wait_ge(prefix_mm.sem, prefix_mm.at(a, 1))
                both = oh[:].rearrange("p (t k) e -> p t k e", k=2)
                for ins in (
                    lambda: dve.tensor_tensor(pos[:], pp[:, 0:TT * E].rearrange("p (t e) -> p t e", e=E),
                                              base[:].unsqueeze(1).to_broadcast([P, TT, E]), ALU.add),
                    lambda: dve.tensor_tensor(base[:], base[:], pp[:, TT * E:TT * E + E], ALU.add),
                    lambda: dve.tensor_tensor(picked[:].rearrange("p (t k) e -> p t k e", k=2), both,
                                              pos[:].unsqueeze(2).to_broadcast([P, TT, 2, E]), ALU.mult),
                    lambda: dve.tensor_reduce(slotf[:], picked[:], AX.X, ALU.add),
                    lambda: dve.tensor_copy(slot[:], slotf[:]),
                    lambda: dve.tensor_copy(keep["slots"][:, bass.ds(a * 2 * TT, 2 * TT)], slotf[:]),
                ):
                    ins().then_inc(route.sem, 1)
                    n += 1
                    dve.wait_ge(route.sem, route.at(a, n))

            def low_x(b):
                for k in range(KD):
                    dve.wait_ge(xT_hi.sem, xT_hi.at(b, k + 1))
                    dve.tensor_tensor(xT[1][:, k, :], xTf[:, k, :], xT[0][:, k, :], ALU.subtract
                                      ).then_inc(xT_lo.sem, 1)

            def add_x1(b, t):
                if t == 0:
                    dve.wait_ge(xb_in.sem, xb_in.at(b, 48))
                dve.wait_ge(out_mm.sem, out_mm.at(b, t + 1))
                dve.tensor_tensor(xb[:, t, :], po[:, t % 2, 0:D], xb[:, t, :], ALU.add).then_inc(out_sb.sem, 1)

            def body(b, second, third, last):
                if second or not last:
                    deviations(b + 1, None if last else b + 1, b - 1 if second else None)
                if second:
                    norm_x2(b - 1)
                for c in range(FMC):
                    if c not in POOLED:
                        dve.wait_ge(hid_hi.sem, hid_hi.at(b, c + 1))
                        dve.tensor_tensor(hd[1][:, c, :], hid[:, c % HB, :], hd[0][:, c, :], ALU.subtract
                                          ).then_inc(hid_lo.sem, 1)
                    if c == 4 and not last:
                        norm_x1(b + 1)
                if third:
                    choose(b - 2)
                add_x1(b, 0)
                if third:
                    place(b - 2)
                if not last:
                    low_x(b + 1)
                add_x1(b, 1)
                for n, (_, area, places) in enumerate(piece(b)):
                    dve.wait_ge(piece_hi.sem, piece_hi.at(b, n + 1))
                    dve.tensor_tensor(places[1], area, places[0], ALU.subtract).then_inc(piece_lo.sem, 1)
                add_x1(b, 2)
                add_x1(b, 3)
                if second:
                    split_rows(b - 1)

            dve.wait_ge(ready.sem, 2)
            deviations(0, 0, None)
            norm_x1(0)
            low_x(0)
            loop(dve, body)
            choose(NB - 2)
            place(NB - 2)
            deviations(NB + 1, None, NB - 1)
            norm_x2(NB - 1)
            split_rows(NB - 1)
            choose(NB - 1)
            place(NB - 1)

        @block.gpsimd
        def _(pool):
            def modulate(a):
                pool.wait_ge(t_norm.sem, t_norm.at(a, 4))
                pool.wait_ge(sh_in.sem, sh_in.at(a, 16))
                for n, (i, op) in enumerate(((1, ALU.mult), (0, ALU.add))):
                    pool.tensor_tensor(h2[:], h2[:], shsc[:, i:i + 1, :].to_broadcast([P, TT, D]), op
                                       ).then_inc(s_h2.sem, 1)
                    pool.wait_ge(s_h2.sem, s_h2.at(a, n + 1))

            def send(a):
                pool.wait_ge(row_lo.sem, row_lo.at(a, 1))
                wait_alone(pool, route.sem, route.at(a, 18), pool_passed)
                for t in range(TT):
                    for k in range(2):
                        pool.indirect_dma_start(
                            out=scratch["queue"], out_offset=bass.IndirectOffsetOnAxis(
                                ap=slot[:, 2 * t + k:2 * t + k + 1], axis=0),
                            in_=rows[:, t, :, :].rearrange("p i d -> p (i d)"), in_offset=None
                        ).then_inc(sent.sem, 16)

            def residual(b):
                pool.wait_ge(x2_out.sem, x2_out.at(b, 0))
                for t in range(TT):
                    pool.wait_ge(out_sb.sem, out_sb.at(b, t + 1))
                    pool.tensor_tensor(xb[:, t, :], xb[:, t, :], ga[:, 0, :], ALU.mult).then_inc(x2_gated.sem, 1)
                    pool.wait_ge(x2_gated.sem, x2_gated.at(b, t + 1))
                    pool.tensor_tensor(x2[:, t, :], xb[:, t, :], x[:, t, :], ALU.add).then_inc(x2_sb.sem, 1)

            def body(b, second, third, last):
                for c in POOLED:
                    pool.wait_ge(hid_hi.sem, hid_hi.at(b, c + 1))
                    pool.tensor_tensor(hd[1][:, c, :], hid[:, c % HB, :], hd[0][:, c, :], ALU.subtract
                                       ).then_inc(hid_lo_pool.sem, 1)
                if second:
                    modulate(b - 1)
                if third:
                    send(b - 2)
                residual(b)

            pool.iota(iota8[:], pattern=[[1, E]], base=0, channel_multiplier=0,
                      allow_small_or_imprecise_dtypes=True).then_inc(ready.sem, 1)
            pool.iota(base[:], pattern=[[capacity, E]], base=0, channel_multiplier=0,
                      allow_small_or_imprecise_dtypes=True).then_inc(ready.sem, 1)
            loop(pool, body)
            send(NB - 2)
            modulate(NB - 1)
            send(NB - 1)
            pool.wait_ge(sent.sem, 16 * 2 * TT * NB)



def plan(nc, keep, scratch, capacity, n_tiles):
    with ExitStack() as ctx:
        m = Memory(nc, ctx, "plan_")
        row = lambda name, n, dt=F32: m.sb(name, [1, n], dt)
        cnt, whole, cum, ones, move, step = (m.sb(n, [P, E]) for n in ("cnt", "whole", "cum", "ones", "move", "step"))
        cnti = m.sb("cnti", [P, E], I32)
        slots = keep["slots"]
        moved = m.sb("moved", list(slots.shape))
        extra = m.sb("extra", list(slots.shape))
        ends = row("ends", E, I32)
        top = row("top", 1)
        tile, ex, before, first = (row(n, n_tiles) for n in ("tile", "ex", "before", "first"))
        ge = m.sb("ge", [1, n_tiles, E])
        gn = m.sb("gn", [1, n_tiles, E])
        start = m.sb("start", [P, E])
        zeros = m.sb("zeros", [P, ROWS // P * 2 * D], F16)
        made = m.counter("made")
        planned = m.counter("planned")
        padded = m.counter("padded")
        block = ctx.enter_context(nc.Block())

        @block.gpsimd
        def _(pool):
            pool.iota(start[:], pattern=[[capacity, E]], base=0, channel_multiplier=0,
                      allow_small_or_imprecise_dtypes=True).then_inc(made.sem, 1)
            pool.iota(tile[:], pattern=[[1, n_tiles]], base=0, channel_multiplier=0,
                      allow_small_or_imprecise_dtypes=True).then_inc(made.sem, 1)
            pool.memset(ones[:], 1.0).then_inc(made.sem, 1)
            pool.memset(zeros[:], 0.0).then_inc(made.sem, 1)

        @block.vector
        def _(dve):
            per_tile = lambda ap: ap[:].unsqueeze(2).to_broadcast([1, n_tiles, E])
            per_expert = lambda ap: ap[0:1, :].unsqueeze(1).to_broadcast([1, n_tiles, E])
            base = keep["base"]
            dve.wait_ge(made.sem, 4)
            for n, ins in enumerate((
                lambda: dve.tensor_copy(ends[:], base[0:1, :]),
                lambda: dve.tensor_tensor(cnt[:], base[:], start[:], ALU.subtract),
                lambda: dve.tensor_scalar(cnti[:], cnt[:], float(ROWS - 1), None, ALU.add),
                lambda: dve.tensor_scalar(cnti[:], cnti[:], ROWS.bit_length() - 1, None, ALU.logical_shift_right),
                lambda: dve.tensor_copy(whole[:], cnti[:]),
                lambda: dve.tensor_tensor_scan(cum[:], ones[:], whole[:], 0.0, ALU.mult, ALU.add),
                lambda: dve.tensor_scalar(top[:], cum[0:1, E - 1:E], -1.0, None, ALU.add),
                lambda: dve.tensor_scalar(tile[:], tile[:], top[:, 0:1], None, ALU.min),
                lambda: dve.tensor_tensor(ge[:], per_tile(tile), per_expert(cum), ALU.is_ge),
                lambda: dve.tensor_reduce(ex[:], ge[:], AX.X, ALU.add),
                lambda: dve.tensor_tensor(gn[:], ge[:], per_expert(whole), ALU.mult),
                lambda: dve.tensor_reduce(before[:], gn[:], AX.X, ALU.add),
                lambda: dve.tensor_tensor(first[:], tile[:], before[:], ALU.subtract),
                lambda: dve.tensor_scalar(first[:], first[:], float(ROWS), None, ALU.mult),
                lambda: dve.scalar_tensor_tensor(out=first[:], in0=ex[:], scalar=float(capacity), in1=first[:],
                                                 op0=ALU.mult, op1=ALU.add),
                lambda: dve.tensor_copy(keep["tiles"][:, 0, :], ex[:]),
                lambda: dve.tensor_copy(keep["tiles"][:, 1, :], first[:]),
                lambda: dve.tensor_tensor(move[:], cum[:], whole[:], ALU.subtract),
                lambda: dve.scalar_tensor_tensor(out=move[:], in0=move[:], scalar=float(ROWS), in1=start[:],
                                                 op0=ALU.mult, op1=ALU.subtract),
                lambda: dve.tensor_tensor(step[:, 1:E], move[:, 1:E], move[:, 0:E - 1], ALU.subtract),
                lambda: dve.tensor_copy(moved[:], slots[:]),
                *(lambda e=e, half=half: (
                    dve.tensor_scalar(extra[:], slots[:], float(e * capacity), step[:, e:e + 1], ALU.is_ge, ALU.mult)
                    if half == 0 else dve.tensor_tensor(moved[:], moved[:], extra[:], ALU.add))
                  for e in range(1, E) for half in range(2)),
                lambda: dve.tensor_copy(keep["rows"][:], moved[:]),
            )):
                ins().then_inc(planned.sem, 1)
                dve.wait_ge(planned.sem, n + 1)

        @block.sync
        def _(sp):
            sp.wait_ge(made.sem, 4)
            sp.wait_ge(planned.sem, 1)
            for e in range(E):
                end = sp.value_load(ends[0:1, e:e + 1], min_val=e * capacity, max_val=(e + 1) * capacity - ROWS)
                sp.dma_start(scratch["queue"][bass.ds(end, ROWS), :].rearrange("(r p) d -> p r d", p=P),
                             zeros[:].rearrange("p (r d) -> p r d", r=ROWS // P)).then_inc(padded.sem, 16)
            sp.wait_ge(padded.sem, 16 * E)


def expert_pieces(din, x, stage):
    half = FC // 2
    w1 = din["x_w1"].rearrange("e (k p) n -> (e k) p n", p=P)
    w2 = din["x_w2"].rearrange("e (h f p) d -> (e h) p f d", p=P, f=half)
    stage1, stage2 = stage[:, 0:2 * F], stage[:, 2 * F:].rearrange("p (f d) -> p f d", f=half)

    def piece(j):
        return ((w1[bass.ds(j, 1), :, :].rearrange("a p n -> (a p) n"), stage1,
                 [a[:, bass.ds(j, 1), :].rearrange("p a n -> p (a n)") for a in x["w1"]]),
                (w2[bass.ds(j, 1), :, :, :].rearrange("a p f d -> (a p) f d"), stage2,
                 [a[:, bass.ds(j, 1), :, :].rearrange("p a f d -> p (a f) d") for a in x["w2"]]))

    return piece


def expert_weights(nc, din, x, first):
    with ExitStack() as inner:
        m = Memory(nc, inner, "xload_")
        stage = m.sb("stage", [P, PIECE])
        loaded, split, split_hi = m.counter("loaded"), m.counter("split"), m.counter("split_hi")
        bias_in, bias_up = m.counter("bias_in"), m.counter("bias_up")
        piece = expert_pieces(din, x, stage)
        jobs = [part for j in range(first, 2 * E) for part in piece(j)]
        block = inner.enter_context(nc.Block())

        @block.sync
        def _(sp):
            sp.dma_start(x["b1"][:], din["x_b1"]).then_inc(bias_in.sem, 16)
            sp.dma_start(x["b2"][:], din["x_b2"].rearrange("(a e) d -> a e d", a=1).to_broadcast([P, E, D])
                         ).then_inc(bias_in.sem, 16)
            for n, (src, area, _) in enumerate(jobs):
                sp.wait_ge(split.sem, max(n - 1, 0))
                sp.dma_start(area, src).then_inc(loaded.sem, 16)
                sp.wait_ge(loaded.sem, 16 * (n + 1))
            sp.wait_ge(bias_in.sem, 32)

        @block.scalar
        def _(act):
            for n, (_, area, places) in enumerate(jobs):
                act.wait_ge(loaded.sem, 16 * (n + 1))
                act.copy(places[0], area).then_inc(split_hi.sem, 1)

        @block.vector
        def _(dve):
            dve.wait_ge(bias_in.sem, 32)
            dve.tensor_scalar(x["b1"][:, :, FC:], x["b1"][:, :, FC:], 1.0, None, ALU.add).then_inc(bias_up.sem, 1)
            for n, (_, area, places) in enumerate(jobs):
                dve.wait_ge(split_hi.sem, n + 1)
                dve.tensor_tensor(places[1], area, places[0], ALU.subtract).then_inc(split.sem, 1)


def experts(nc, w, x, keep, scratch, capacity, n_tiles):
    RT = ROWS // P
    last_row = (E * capacity) - ROWS
    with ExitStack() as ctx:
        m = Memory(nc, ctx, "experts_")
        rows = m.sb("rows", [P, 2, RT, 2 * D], F16)
        xT = m.sb("xT", [P, 2, 2, KD, ROWS], F16)
        g = m.sb("g", [P, 2, 2 * ROWS])
        sg = m.sb("sg", [P, 2, 2 * ROWS])
        v = m.sb("v", [P, 2, 2 * ROWS])
        hf = m.sb("hf", [P, 2, 2 * ROWS])
        h = [m.sb(n, [P, 2, FC, ROWS], F16) for n in ("hh", "hl")]
        y = m.sb("y", [P, 2, RT, D])
        pt = m.ps("pt", [P, 2 * KD, ROWS], F16)
        pg = m.ps("pg", [P, 2, 512])
        pv = m.ps("pv", [P, 2, 512])
        py = m.ps("py", [P, 2, 512])
        row_in = [m.counter(f"row_in{u}", 16) for u in range(2)]
        turned = m.counter("turned", 1)
        xT_sb = m.counter("xT_sb", 1)
        up_mm = m.counter("up_mm", 2)
        g_sb, v_sb = m.counter("g_sb", 4), m.counter("v_sb", 4)
        sig_sb, gs = m.counter("sig_sb", 2), m.counter("gs", 2)
        h_f, h_hi, h_lo = m.counter("h_f", 2), m.counter("h_hi", 2), m.counter("h_lo", 2)
        down_mm = m.counter("down_mm", 1)
        y_sb = m.counter("y_sb", 1)
        y_out = [m.counter(f"y_out{u}", 16) for u in range(2)]
        block = ctx.enter_context(nc.Block())

        def loop(eng, body):
            for i in range(2):
                for u in range(2):
                    body(i, u, i + u == 0, False)
            with eng.Fori(2, n_tiles // 2 - 1) as i:
                for u in range(2):
                    body(i, u, False, False)
            for u in range(2):
                body(n_tiles // 2 - 1, u, False, True)

        def expert_of(eng, tile):
            return eng.value_load(keep["tiles"][0:1, 0, bass.ds(tile, 1)], min_val=0, max_val=E - 1)

        def row_of(eng, tile):
            return eng.value_load(keep["tiles"][0:1, 1, bass.ds(tile, 1)], min_val=0, max_val=last_row)

        def flat(ap, u, q):
            return ap[:, u, 2 * q:2 * q + 2, :].rearrange("p f r -> p (f r)")

        @block.sync
        def _(sp):
            def load(tile, u):
                r = row_of(sp, tile)
                sp.dma_start(rows[:, u, :, :], scratch["queue"][bass.ds(r, ROWS), :].rearrange(
                    "(t p) d -> p t d", p=P)).then_inc(row_in[u].sem, 16)

            def store(tile, u):
                sp.wait_ge(y_sb.sem, y_sb.at(tile, 1))
                sp.dma_start(scratch["y"][bass.ds(tile * ROWS, ROWS), :].rearrange("(t p) d -> p t d", p=P),
                             y[:, u, :, :]).then_inc(y_out[u].sem, 16)

            def body(pair, u, first, ending):
                tile = pair * 2 + u
                if not ending:
                    sp.wait_ge(turned.sem, turned.at(tile, 1))
                    load(tile + 2, u)
                if not (isinstance(pair, int) and pair == 0):
                    store(tile - 2, u)

            load(0, 0)
            load(1, 1)
            loop(sp, body)
            store(n_tiles - 2, 0)
            store(n_tiles - 1, 1)
            for u in range(2):
                sp.wait_ge(y_out[u].sem, y_out[u].at(n_tiles // 2, 0))

        @block.tensor
        def _(pe):
            def turn(pair, u):
                tile = pair * 2 + u
                pe.wait_ge(row_in[u].sem, row_in[u].at(pair, 16))
                pe.wait_ge(xT_sb.sem, xT_sb.at(tile, 0))
                for t in range(RT):
                    for i in range(2):
                        for k in range(KD):
                            last = pe.transpose(pt[:, i * KD + k, t * P:(t + 1) * P],
                                                rows[:, u, t, (i * KD + k) * P:(i * KD + k + 1) * P],
                                                w["identh"][:])
                last.then_inc(turned.sem, 1)

            def up(tile, u, e):
                pe.wait_ge(xT_sb.sem, xT_sb.at(tile, 1))
                for q in range(2):
                    pe.wait_ge(g_sb.sem, g_sb.at(tile - 1, 2 * q + 2))
                    pe.wait_ge(v_sb.sem, v_sb.at(tile - 1, 2 * q + 2))
                    for part, bank in ((0, pg), (1, pv)):
                        for f in range(2):
                            col = part * F + (2 * q + f) * P
                            for k in range(KD):
                                last = hi_lo_products(
                                    pe, bank[:, q, f * ROWS:(f + 1) * ROWS],
                                    [a[:, bass.ds(e * KD + k, 1), col:col + P].rearrange("p a n -> p (a n)")
                                     for a in x["w1"]],
                                    [xT[:, u, i, k, :] for i in range(2)], k == 0, k == KD - 1)
                    last.then_inc(up_mm.sem, 1)

            def down(tile, u, e):
                pe.wait_ge(h_lo.sem, h_lo.at(tile, 2))
                pe.wait_ge(y_sb.sem, y_sb.at(tile - 1, 0))
                for t in range(RT):
                    for f in range(FC):
                        last = hi_lo_products(
                            pe, py[:, u, t * D:(t + 1) * D], [a[:, u, f, t * P:(t + 1) * P] for a in h],
                            [a[:, bass.ds(e * 2 + f // 2, 1), f % 2, :].rearrange("p a n -> p (a n)") for a in x["w2"]],
                            f == 0, f == FC - 1)
                last.then_inc(down_mm.sem, 1)

            def body(pair, u, first, ending):
                tile = pair * 2 + u
                e_up = expert_of(pe, tile)
                e_down = None if first else expert_of(pe, tile - 1)
                up(tile, u, e_up)
                if not ending:
                    turn(pair + 1, u)
                if not first:
                    down(tile - 1, 1 - u, e_down)

            turn(0, 0)
            turn(0, 1)
            loop(pe, body)
            down(n_tiles - 1, 1, expert_of(pe, n_tiles - 1))

        @block.scalar
        def _(act):
            def copy_rows(tile, u):
                act.wait_ge(turned.sem, turned.at(tile, 1))
                act.copy(xT[:, u, :, :, :].rearrange("p i k r -> p (i k) r"), pt[:]).then_inc(xT_sb.sem, 1)

            def body(pair, u, first, ending):
                tile = pair * 2 + u

                def sigmoid(q):
                    act.wait_ge(h_f.sem, h_f.at(tile - 1, q + 1))
                    act.wait_ge(g_sb.sem, g_sb.at(tile, 2 * q + 2))
                    act.activation(sg[:, q, :], g[:, q, :], ACT.Sigmoid, scale=1.702).then_inc(sig_sb.sem, 1)

                def high(q):
                    act.wait_ge(down_mm.sem, down_mm.at(tile - 1, 0))
                    act.wait_ge(h_f.sem, h_f.at(tile, q + 1))
                    act.copy(flat(h[0], u, q), hf[:, q, :]).then_inc(h_hi.sem, 1)

                sigmoid(0)
                sigmoid(1)
                high(0)
                if not ending:
                    copy_rows(tile + 2, u)
                high(1)

            copy_rows(0, 0)
            copy_rows(1, 1)
            loop(act, body)

        @block.vector
        def _(dve):
            def body(pair, u, first, ending):
                tile = pair * 2 + u
                e = expert_of(dve, tile)

                def gates_and_values(q):
                    dve.wait_ge(gs.sem, gs.at(tile - 1, q + 1))
                    dve.wait_ge(h_f.sem, h_f.at(tile - 1, q + 1))
                    dve.wait_ge(up_mm.sem, up_mm.at(tile, q + 1))
                    for dst, bank, bias, top, done in ((g, pg, 0, 9.0, g_sb), (v, pv, FC, 10.0, v_sb)):
                        for f in range(2):
                            dve.tensor_scalar(dst[:, q, f * ROWS:(f + 1) * ROWS], bank[:, q, f * ROWS:(f + 1) * ROWS],
                                              x["b1"][:, bass.ds(e, 1), bias + 2 * q + f], top, ALU.add, ALU.min
                                              ).then_inc(done.sem, 1)

                def hidden(q):
                    dve.wait_ge(gs.sem, gs.at(tile, q + 1))
                    dve.wait_ge(v_sb.sem, v_sb.at(tile, 2 * q + 2))
                    dve.wait_ge(h_lo.sem, h_lo.at(tile - 1, q + 1))
                    dve.scalar_tensor_tensor(out=hf[:, q, :], in0=v[:, q, :], scalar=-8.0, in1=sg[:, q, :],
                                             op0=ALU.max, op1=ALU.mult).then_inc(h_f.sem, 1)

                def low(q):
                    dve.wait_ge(h_hi.sem, h_hi.at(tile, q + 1))
                    dve.tensor_tensor(flat(h[1], u, q), hf[:, q, :], flat(h[0], u, q), ALU.subtract
                                      ).then_inc(h_lo.sem, 1)

                gates_and_values(0)
                gates_and_values(1)
                hidden(0)
                if not first:
                    add_bias(pair - 1 + u, tile - 1, 1 - u)
                low(0)
                hidden(1)
                low(1)

            def add_bias(pair, tile, u):
                e = expert_of(dve, tile)
                dve.wait_ge(down_mm.sem, down_mm.at(tile, 1))
                dve.wait_ge(y_out[u].sem, y_out[u].at(pair, 0))
                dve.tensor_tensor(y[:, u, :, :], py[:, u, :].rearrange("p (t d) -> p t d", t=RT),
                                  x["b2"][:, bass.ds(e, 1), :].to_broadcast([P, RT, D]), ALU.add
                                  ).then_inc(y_sb.sem, 1)

            loop(dve, body)
            add_bias(n_tiles // 2 - 1, n_tiles - 1, 1)

        @block.gpsimd
        def _(pool):
            def body(pair, u, first, ending):
                tile = pair * 2 + u
                for q in range(2):
                    pool.wait_ge(sig_sb.sem, sig_sb.at(tile, q + 1))
                    pool.tensor_tensor(sg[:, q, :], sg[:, q, :], g[:, q, :], ALU.mult).then_inc(gs.sem, 1)

            loop(pool, body)



def combine(nc, din, keep, scratch, out, NB):
    with ExitStack() as ctx:
        m = Memory(nc, ctx, "combine_")
        n_pairs = NB * TT
        p = m.sb("p", [P, n_pairs, 2])
        total = m.sb("total", [P, n_pairs])
        slot = m.sb("slot", [P, 2, 2 * TT], I32)
        pb = m.sb("pb", [P, 2, 2 * TT])
        y = m.sb("y", [P, 2, 2 * TT, D])
        x2 = m.sb("x2", [P, 2, TT, D])
        gb = m.sb("gb", [P, 2, 1, D])
        acc = m.sb("acc", [P, 2, TT, D])
        shifted, exped, weighed = m.counter("shifted"), m.counter("exped"), m.counter("weighed")
        passed = m.counter("passed")
        by_parity = lambda name, per: [m.counter(f"{name}{u}", per) for u in range(2)]
        x2_in = by_parity("x2_in", 32)
        slot_sb = by_parity("slot_sb", 1)
        y_in = by_parity("y_in", 16 * 2 * TT)
        p_sb = by_parity("p_sb", 1)
        first, both = by_parity("first", TT), by_parity("both", TT)
        gated, summed = by_parity("gated", 1), by_parity("summed", 1)
        out_done = by_parity("out_done", 16)
        block = ctx.enter_context(nc.Block())

        def loop(eng, body):
            for u in range(2):
                body(0, u, u)
            if NB > 4:
                with eng.Fori(1, NB // 2 - 1) as pair:
                    for u in range(2):
                        body(pair, u, pair * 2 + u)
            for u in range(2):
                body(NB // 2 - 1, u, NB - 2 + u)

        def rows_of(ap, b):
            return ap[bass.ds(b, 1), :, :].rearrange("a (t p) d -> p (a t) d", p=P)

        @block.sync
        def _(sp):
            def load(pair, u, b):
                sp.wait_ge(summed[u].sem, summed[u].at(pair, 0))
                sp.dma_start(x2[:, u, :, :], rows_of(scratch["x2"], b)).then_inc(x2_in[u].sem, 16)
                sp.dma_start(gb[:, u, :, :], scratch["mod"][bass.ds(b, 1), 5 * D:6 * D].rearrange(
                    "a (i d) -> a i d", i=1).to_broadcast([P, 1, D])).then_inc(x2_in[u].sem, 16)

            loop(sp, load)

        @block.scalar
        def _(act):
            act.wait_ge(shifted.sem, 1)
            act.activation(p[:], p[:], ACT.Exp).then_inc(exped.sem, 1)

            def store(pair, u, b):
                act.wait_ge(summed[u].sem, summed[u].at(pair, 1))
                act.dma_start(rows_of(out, b), acc[:, u, :, :]).then_inc(out_done[u].sem, 16)

            loop(act, store)
            for u in range(2):
                act.wait_ge(out_done[u].sem, out_done[u].at(NB // 2, 0))

        @block.gpsimd
        def _(pool):
            def gather(pair, u, b):
                pool.wait_ge(both[u].sem, both[u].at(pair, 0))
                pool.tensor_copy(slot[:, u, :], keep["rows"][:, bass.ds(b * 2 * TT, 2 * TT)]
                                 ).then_inc(slot_sb[u].sem, 1)
                wait_alone(pool, slot_sb[u].sem, slot_sb[u].at(pair, 1), passed)
                for j in range(2 * TT):
                    pool.indirect_dma_start(out=y[:, u, j, :], out_offset=None, in_=scratch["y"],
                                            in_offset=bass.IndirectOffsetOnAxis(ap=slot[:, u, j:j + 1], axis=0)
                                            ).then_inc(y_in[u].sem, 16)

            loop(pool, gather)

        @block.vector
        def _(dve):
            lead = keep["top"][:, :, 0:1].to_broadcast([P, n_pairs, 2])
            dve.tensor_tensor(p[:], keep["top"][:], lead, ALU.subtract).then_inc(shifted.sem, 1)
            dve.wait_ge(exped.sem, 1)
            dve.tensor_reduce(total[:], p[:], AX.X, ALU.add).then_inc(weighed.sem, 1)
            dve.wait_ge(weighed.sem, 1)
            dve.reciprocal(total[:], total[:]).then_inc(weighed.sem, 1)
            dve.wait_ge(weighed.sem, 2)
            dve.tensor_tensor(p[:], p[:], total[:].unsqueeze(2).to_broadcast([P, n_pairs, 2]), ALU.mult
                              ).then_inc(weighed.sem, 1)
            dve.wait_ge(weighed.sem, 3)

            def blend(pair, u, b):
                dve.wait_ge(both[u].sem, both[u].at(pair, 0))
                dve.tensor_copy(pb[:, u, :].rearrange("p (t k) -> p t k", k=2), p[:, bass.ds(b * TT, TT), :]
                                ).then_inc(p_sb[u].sem, 1)
                dve.wait_ge(p_sb[u].sem, p_sb[u].at(pair, 1))
                dve.wait_ge(y_in[u].sem, y_in[u].at(pair + 1, 0))
                dve.wait_ge(out_done[u].sem, out_done[u].at(pair, 0))
                for t in range(TT):
                    dve.tensor_scalar(acc[:, u, t, :], y[:, u, 2 * t, :], pb[:, u, 2 * t:2 * t + 1], None, ALU.mult
                                      ).then_inc(first[u].sem, 1)
                for t in range(TT):
                    dve.wait_ge(first[u].sem, first[u].at(pair, t + 1))
                    dve.scalar_tensor_tensor(out=acc[:, u, t, :], in0=y[:, u, 2 * t + 1, :],
                                             scalar=pb[:, u, 2 * t + 1:2 * t + 2], in1=acc[:, u, t, :],
                                             op0=ALU.mult, op1=ALU.add).then_inc(both[u].sem, 1)
                dve.wait_ge(both[u].sem, both[u].at(pair + 1, 0))
                dve.wait_ge(x2_in[u].sem, x2_in[u].at(pair + 1, 0))
                dve.tensor_tensor(acc[:, u, :, :], acc[:, u, :, :], gb[:, u, :, :].to_broadcast([P, TT, D]), ALU.mult
                                  ).then_inc(gated[u].sem, 1)
                dve.wait_ge(gated[u].sem, gated[u].at(pair, 1))
                dve.tensor_tensor(acc[:, u, :, :], acc[:, u, :, :], x2[:, u, :, :], ALU.add
                                  ).then_inc(summed[u].sem, 1)

            loop(dve, blend)


def n_tiles(NB):
    n = 2 * NB * L // ROWS + E - 1
    return n + n % 2


def program(nc, din, out, scratch, NB):
    capacity = NB * L + ROWS
    with ExitStack() as ctx:
        m = Memory(nc, ctx, "w_")
        w = {}
        keep = {"base": m.sb("base", [P, E]), "top": m.sb("top", [P, NB * TT, 2]),
                "slots": m.sb("slots", [P, NB * 2 * TT]), "rows": m.sb("rows", [P, NB * 2 * TT], I32),
                "tiles": m.sb("tiles", [1, 2, n_tiles(NB)], I32)}

        def const(name, shape, dt=F32):
            w[name] = m.sb(name, shape, dt)

        def halves(name, k, n):
            w[name] = [m.sb(f"{name}_{part}", [P, k, n], F16) for part in ("hi", "lo")]

        const("identf", [P, P])
        const("identb", [P, P], BF16)
        const("identh", [P, P], F16)
        with ExitStack() as dense:
            m = Memory(nc, dense, "w_")
            halves("gate", KD, E)
            const("ones3", [3, P], BF16)
            const("ones", [P, P], BF16)
            const("before", [P, P], BF16)
            const("b23", [3, D], BF16)
            for name, k in (("g1", KD), ("b1", KD), ("g2", KD), ("b2", KD), ("mb1", FMC), ("bu", 1), ("A", 1)):
                const(name, [P, k])
            halves("w1", KD, FM)
            halves("w2", FMC, D)
            with ExitStack() as mixer_only:
                m = Memory(nc, mixer_only, "w_")
                halves("qk", KD, 2 * D)
                halves("v", KD, D)
                halves("g", KD, D)
                halves("drive", KD, S)
                halves("o", 2, D)
                halves("c", 1, D)
                halves("nc", 1, D)
                for name in ("bg3", "bo3"):
                    const(name, [3, D], BF16)
                const("twoI", [P, P], BF16)
                const("parity", [P, 2])
                const("maskq", [P, 2, 4, P], BF16)
                const("select", [P, 2, PAIRS, P], BF16)
                const("shift", [P, 2, P], BF16)
                const("mx", [P, 2, P], BF16)
                for name in ("xTh", "xTl"):
                    const(name, [P, KD, WIN + L], F16)
                const("Kz", [P, 4, 2, 2, WIN + L], F16)
                const("V", [P, NW, PAIRS, 2 * DH + 1])
                setup(nc, din, w, scratch)
                mixer(nc, din, w, scratch, NB)
            m = Memory(nc, dense, "x_")
            x = {"w1": [m.sb(f"w1{i}", [P, 2 * E, 2 * F], F16) for i in range(2)],
                 "w2": [m.sb(f"w2{i}", [P, 2 * E, FC // 2, D], F16) for i in range(2)],
                 "b1": m.sb("b1", [P, E, 2 * FC]), "b2": m.sb("b2", [P, E, D])}
            mlp(nc, din, w, x, scratch, NB, keep, capacity)
            plan(nc, keep, scratch, capacity, n_tiles(NB))
            expert_weights(nc, din, x, NB)
            experts(nc, w, x, keep, scratch, capacity, n_tiles(NB))
        combine(nc, din, keep, scratch, out, NB)


def launch_arrays(inputs):
    import numpy as np

    a = {name.removeprefix("L0_").removeprefix("attn_"): np.asarray(v) for name, v in inputs.items()}
    column = lambda v, k: v.reshape(k, P).T
    NB = a["x"].shape[0]
    w1 = a["ffn_dense_1_w"].transpose(0, 2, 1)
    b1 = a["ffn_dense_1_b"]
    arrays = {
        "x": a["x"], "cT": a["c"].T.reshape(KD, P, NB).transpose(1, 0, 2), "wmod": a["wmod"],
        "Wqk": a["W_qkv"][:, :2 * D], "Wv": a["W_qkv"][:, 2 * D:], "Wu": a["W_ug"][:, :S], "Wg": a["W_ug"][:, S:],
        "b_u": column(a["b_ug"][:S], 1), "b_g": a["b_ug"][S:], "Bw": a["B_w"], "A": column(a["A"], 1),
        "Cw": a["C_w"], "b_O": a["b_O"],
        "WO": a["W_O"].reshape(PAIRS, 2, DH, D).transpose(1, 0, 2, 3).reshape(D, D),
        "ln1_g": column(a["ln1_g"], KD), "ln1_b": column(a["ln1_b"], KD),
        "ln2_g": column(a["ln2_g"], KD), "ln2_b": column(a["ln2_b"], KD),
        "W1": a["mlp_W1"], "mlp_b1": column(a["mlp_b1"], FMC), "W2": a["mlp_W2"], "mlp_b2": a["mlp_b2"],
        "gate_w": a["ffn_gate_w"],
        "x_w1": np.concatenate([w1[:, :, 0::2], w1[:, :, 1::2]], 2),
        "x_b1": np.concatenate([b1[:, 0::2], b1[:, 1::2]], 1).reshape(E, 2 * FC, P).transpose(2, 0, 1),
        "x_w2": a["ffn_dense_2_w"].transpose(0, 2, 1), "x_b2": a["ffn_dense_2_b"],
    }
    return {name: np.ascontiguousarray(v) for name, v in arrays.items()}


def build(nc, arrays):
    NB = arrays["x"].shape[0]
    capacity = NB * L + ROWS
    din = {n: nc.dram_tensor(f"in_{n}", v.shape, mybir.dt.from_np(v.dtype), kind="ExternalInput").ap()
           for n, v in arrays.items()}
    out = nc.dram_tensor("out", (NB, L, D), F32, kind="ExternalOutput").ap()
    scratch = {}
    for name, shape, dt in (("mod", (NB, 6 * D), F32), ("x1", (NB, L, D), F32), ("x2", (NB, L, D), F32),
                            ("queue", (E * capacity, 2 * D), F16), ("y", (n_tiles(NB) * ROWS, D), F32)):
        scratch[name] = nc.dram_tensor(f"scratch_{name}", shape, dt).ap()
    program(nc, din, out, scratch, NB)


def kernel(**inputs):
    import concourse.bacc as _bacc
    from concourse.bass_utils import run_bass_kernel_spmd as _run

    nc = _bacc.Bacc("TRN2", target_bir_lowering=False, num_devices=1)
    arrays = launch_arrays(inputs)
    build(nc, arrays)
    r = _run(nc, [{f"in_{n}": v for n, v in arrays.items()}], core_ids=[0])
    return r.results[0]["out"]
```
